# Optimizing a Trainium2 kernel written in Bass

```python
import numpy as np
import jax
import jax.numpy as jnp

def _softmax(x, axis=-1):
    return jax.nn.softmax(x, axis=axis)

def _gelu(x):
    return jax.nn.gelu(x, approximate=True)

def _silu(x):
    return jax.nn.silu(x)

def _sigmoid(x):
    return jax.nn.sigmoid(x)

def _layernorm(x, axis=-1, eps=1e-05):
    m = jnp.mean(x, axis=axis, keepdims=True)
    v = jnp.var(x, axis=axis, keepdims=True)
    return (x - m) / jnp.sqrt(v + eps)

def _scatter_add(tgt, idx, src, axis=0):
    return tgt.at[idx].add(src)

def _segment_sum(src, seg, n):
    return jax.ops.segment_sum(src, seg, n)
kernel_name = 'mk_flamingo_gated_d1_seqx_r4_1da69b'

def setup_inputs(seed: int=0):
    np.random.seed(seed)
    _w = jnp.asarray

    def _rec_inputs():
        import jax
        import jax.numpy as jnp
        _rk = jax.random.key(seed)
        x = -7.109e-05 + 0.9999 * jax.random.normal(jax.random.fold_in(_rk, 1), (4, 512, 512), jnp.float32)
        _lenS = 512 - jax.random.randint(jax.random.fold_in(_rk, 7), (4,), 0, max(1, 512 // 4) + 1, jnp.int32)
        _lenS2 = 512 - jax.random.randint(jax.random.fold_in(_rk, 8), (4,), 0, max(1, 512 // 4) + 1, jnp.int32)
        _ctx_512P = jax.random.normal(jax.random.fold_in(_rk, 11), (4, 16, 128), jnp.float32)
        _ctx_512c = jax.random.dirichlet(jax.random.fold_in(_rk, 511), 0.3 * jnp.ones((16,), jnp.float32), (4, 512))
        _ctx_512t = jnp.einsum('bsk,bkd->bsd', _ctx_512c, _ctx_512P)
        _ctx_512t = _ctx_512t * jax.lax.rsqrt(jnp.mean(jnp.square(_ctx_512t)) + 1e-12) * 0.953939
        ctx_512 = 2.81802e-05 + 1.00001 * (_ctx_512t + 0.3 * jax.random.normal(jax.random.fold_in(_rk, 611), (4, 512, 128), jnp.float32))
        _g = jax.random.normal(jax.random.fold_in(_rk, 9001), (2, 1), jnp.float32)
        _g = jnp.sign(_g) * jnp.maximum(jnp.abs(_g), 1.0) + (_g == 0) * 1.0
        g_xattn = _g[0]
        g_ffn = _g[1]
        return (x, ctx_512, g_xattn, g_ffn)
    x, ctx_512, g_xattn, g_ffn = _rec_inputs()

    def _L0_xattn_setup():
        import jax, jax.numpy as jnp
        import numpy as np
        EPS = 1e-06
        IMAGE_DIMS = 512
        key = jax.random.key(seed)
        k1, k2, k3 = jax.random.split(key, 3)
        B, I, J, D = (16, 512, 512, 128)
        p = jax.random.normal(k1, (B, I, J), dtype=jnp.float32)
        k_v = jax.random.normal(k2, (B, J, D), dtype=jnp.float32)
        W_k = jax.random.normal(k3, (D, D), dtype=jnp.float32) * (1.0 / np.sqrt(D))
        b_k = jnp.zeros((D,), dtype=jnp.float32)
        ln_gamma = jnp.ones((J,), dtype=jnp.float32)
        ln_beta = jnp.zeros((J,), dtype=jnp.float32)
        return {'p': p, 'k_v': k_v, 'W_k': W_k, 'b_k': b_k, 'ln_gamma': ln_gamma, 'ln_beta': ln_beta}
    _L0_xattn_all = _L0_xattn_setup()
    _L0_xattn_in = {k: v for k, v in _L0_xattn_all.items() if k in ('W_k', 'b_k', 'ln_gamma', 'ln_beta')}
    del _L0_xattn_all

    def _L0_ffn_setup():
        import jax, jax.numpy as jnp
        import numpy as np
        TOP_K = 2
        CAPACITY_FACTOR = 1.0

        def _ffn(x, w1, w2):
            h = x @ w1
            x1, x2 = jnp.split(h, 2, axis=-1)
            return x1 * jax.nn.silu(x2) @ w2
        key = jax.random.key(seed)
        ks = jax.random.split(key, 6)
        B, S, D, F, E_r, E_s = (4, 512, 512, 256, 7, 1)
        sc_in = 1.0 / np.sqrt(D)
        sc_mid = 1.0 / np.sqrt(F)
        return {'x': jax.random.normal(ks[0], (B, S, D), dtype=jnp.float32), 'gate_w': jax.random.normal(ks[1], (D, E_r), dtype=jnp.float32) * sc_in, 'expert_bias': jnp.zeros((E_r,), dtype=jnp.float32), 'shared_w1': jax.random.normal(ks[2], (E_s, D, 2 * F), dtype=jnp.float32) * sc_in, 'shared_w2': jax.random.normal(ks[3], (E_s, F, D), dtype=jnp.float32) * sc_mid, 'routed_w1': jax.random.normal(ks[4], (E_r, D, 2 * F), dtype=jnp.float32) * sc_in, 'routed_w2': jax.random.normal(ks[5], (E_r, F, D), dtype=jnp.float32) * sc_mid}
    _L0_ffn_all = _L0_ffn_setup()
    _L0_ffn_in = {k: v for k, v in _L0_ffn_all.items() if k in ('gate_w', 'expert_bias', 'shared_w1', 'shared_w2', 'routed_w1', 'routed_w2')}
    del _L0_ffn_all
    return {'x': x, 'ctx_512': ctx_512, 'g_xattn': g_xattn, 'g_ffn': g_ffn, 'L0_xattn_W_k': _L0_xattn_in['W_k'], 'L0_xattn_b_k': _L0_xattn_in['b_k'], 'L0_xattn_ln_gamma': _L0_xattn_in['ln_gamma'], 'L0_xattn_ln_beta': _L0_xattn_in['ln_beta'], 'L0_ffn_gate_w': _L0_ffn_in['gate_w'], 'L0_ffn_expert_bias': _L0_ffn_in['expert_bias'], 'L0_ffn_shared_w1': _L0_ffn_in['shared_w1'], 'L0_ffn_shared_w2': _L0_ffn_in['shared_w2'], 'L0_ffn_routed_w1': _L0_ffn_in['routed_w1'], 'L0_ffn_routed_w2': _L0_ffn_in['routed_w2']}

def reference(x, ctx_512, g_xattn, g_ffn, L0_xattn_W_k, L0_xattn_b_k, L0_xattn_ln_gamma, L0_xattn_ln_beta, L0_ffn_gate_w, L0_ffn_expert_bias, L0_ffn_shared_w1, L0_ffn_shared_w2, L0_ffn_routed_w1, L0_ffn_routed_w2):
    import jax
    import jax.numpy as jnp

    def _L0_xattn_ref(p, k_v, W_k, b_k, ln_gamma, ln_beta):
        import jax, jax.numpy as jnp
        import numpy as np
        EPS = 1e-06
        IMAGE_DIMS = 512
        kv = k_v @ W_k.T + b_k
        out = jnp.einsum('bij,bjd->bid', p, kv)
        scale = IMAGE_DIMS ** (-0.5)
        sim = jnp.einsum('bid,bjd->bij', out, kv) * scale
        mu = jnp.mean(sim, axis=-1, keepdims=True)
        var = jnp.var(sim, axis=-1, keepdims=True)
        sim = (sim - mu) * jax.lax.rsqrt(var + EPS) * ln_gamma + ln_beta
        attn = jax.nn.softmax(sim, axis=-1)
        return attn

    def _L0_ffn_ref(x, gate_w, expert_bias, shared_w1, shared_w2, routed_w1, routed_w2):
        import jax, jax.numpy as jnp
        import numpy as np
        TOP_K = 2
        CAPACITY_FACTOR = 1.0

        def _ffn(x, w1, w2):
            h = x @ w1
            x1, x2 = jnp.split(h, 2, axis=-1)
            return x1 * jax.nn.silu(x2) @ w2
        B, S, D = x.shape
        E_r = gate_w.shape[1]
        T = B * S
        capacity = max(1, int(CAPACITY_FACTOR * T / E_r))
        flat_x = x.reshape(T, D)
        shared_sum = jax.vmap(_ffn, in_axes=(None, 0, 0))(flat_x, shared_w1, shared_w2).sum(0)
        gate_logits = flat_x @ gate_w + expert_bias
        aff = jax.nn.sigmoid(gate_logits)
        _, topk_idx = jax.lax.top_k(aff, TOP_K)
        mask = (topk_idx[:, :, None] == jnp.arange(E_r)[None, None, :]).any(axis=1)
        score = jnp.where(mask, aff, -1.0).T
        _, sel_idx = jax.lax.top_k(score, capacity)
        kept = jnp.take_along_axis(mask.T, sel_idx, axis=1)
        w = jnp.where(kept, jnp.take_along_axis(aff.T, sel_idx, axis=1), 0.0)
        inp = flat_x[sel_idx]
        out = jax.vmap(_ffn)(inp, routed_w1, routed_w2)
        routed_sum = jnp.zeros_like(flat_x).at[sel_idx].add(out * w[:, :, None])
        return (shared_sum + routed_sum).reshape(B, S, D)
    x = x + jnp.tanh(g_xattn[0]) * _L0_xattn_ref(_layernorm(x, axis=-1), ctx_512, L0_xattn_W_k, L0_xattn_b_k, L0_xattn_ln_gamma, L0_xattn_ln_beta)
    x = x + jnp.tanh(g_ffn[0]) * _L0_ffn_ref(_layernorm(x, axis=-1), L0_ffn_gate_w, L0_ffn_expert_bias, L0_ffn_shared_w1, L0_ffn_shared_w2, L0_ffn_routed_w1, L0_ffn_routed_w2)
    return x

_drawn_inputs = setup_inputs


def setup_inputs(seed=0):
    import zlib

    import numpy as np

    out = dict(_drawn_inputs(seed))
    spreads = {'L0_xattn_b_k': (0.0, 2.0),
     'L0_xattn_ln_gamma': (1.0, 0.6),
     'L0_xattn_ln_beta': (0.0, 2.0),
     'L0_ffn_expert_bias': (0.0, 0.1)}
    factors = {'L0_xattn_W_k': 4.323}
    for name, (base, spread) in spreads.items():
        noise = np.random.default_rng([zlib.crc32(name.encode()), seed]).standard_normal(out[name].shape)
        drawn = base * np.exp(spread * noise) if base else spread * noise
        out[name] = jnp.asarray(drawn.astype(out[name].dtype))
    for name, factor in factors.items():
        out[name] = (out[name] * factor).astype(out[name].dtype)
    return out
```

```python
from contextlib import ExitStack

import numpy as np
import concourse.bass as bass
from concourse import mybir

F32 = mybir.dt.float32
F32R = mybir.dt.float32r
BF16 = mybir.dt.bfloat16
I32 = mybir.dt.int32
U32 = mybir.dt.uint32
ALU = mybir.AluOpType
ACT = mybir.ActivationFunctionType
AX = mybir.AxisListType

P = 128
NB = 4
S = 512
D = 512
C = 128
T = NB * S
TT = S // P
NT = T // P
KD = D // P
F = 256
E = 7
CAP = T // E
GE = -(-CAP // P)
GSZ = [min(P, CAP - g * P) for g in range(GE)]
SIM_SCALE2 = 512.0
EPS_SIM = 1e-6
EPS_LN = 1e-5
UNMASKED = -1e30
DIGIT = 4
ROUNDS = 32 // DIGIT
CAND = 2 ** DIGIT - 1
W1N, W2N = KD, 2
NV = 5


def build(nc, x, ctx_in, g_x, g_f, W_k, b_k, gamma, beta, gate_w, ebias, sw1, sw2, rw1, rw2, out):
    with ExitStack() as stack:
        def alloc(where, name, shape, dt=F32):
            return where.enter_context(nc.sbuf_tensor(name, shape, dt))

        def sb(name, shape, dt=F32):
            return alloc(stack, name, shape, dt)

        def pair(where, name, shape):
            return [alloc(where, f"{name}_{part}", shape, F32R) for part in ("hi", "lo")]

        def sem(name):
            return stack.enter_context(nc.semaphore(name))

        bank = [stack.enter_context(nc.psum_tensor(f"bank{i}", [P, 512], F32)) for i in range(8)]
        h_dram = nc.dram_tensor("h_rows", [T, D], F32, kind="Internal").ap()

        ident = sb("ident", [P, P])
        lower = sb("lower", [P, P], BF16)
        ones = sb("ones", [P, P], BF16)
        WkT = sb("WkT", [P, C])
        bk_col = sb("bk_col", [P, 1])
        gates = sb("gates", [P, 2])
        gt = sb("gt", [P, 2])
        eb = sb("eb", [P, E])
        w1_raw = sb("w1_raw", [P, KD, 2 * F])
        w2_raw = sb("w2_raw", [P, 2, D])
        w1s = pair(stack, "w1s", [P, KD, 2 * F])
        w2s = pair(stack, "w2s", [P, 2, D])
        w1r = [pair(stack, "w1r0", [P, KD, 2 * F])]
        w2r = [pair(stack, "w2r0", [P, 2, D])]
        xs = sb("xs", [P, NT, D])
        hT = pair(stack, "hT", [P, KD, S])
        th = sb("th", [P, 2, S])
        gf = sb("gf", [P, 2, S])
        gT = pair(stack, "gT", [P, 2, S])
        z = sb("z", [P, E, NT])
        zs = sb("zs", [P, E, NT])
        z2 = sb("z2", [P, E, NT])
        m1 = sb("m1", [P, NT])
        eq = sb("eq", [P, E, NT])
        key = sb("key", [P, E, NT])
        one1 = sb("one1", [P, E, NT])
        one2 = sb("one2", [P, E, NT])
        mask = sb("mask", [P, E, NT])
        pref = sb("pref", [P, E, 1])
        prefi = sb("prefi", [P, E, 1], I32)
        wt = sb("wt", [P, E, NT])
        thr = sb("thr", [P, E], I32)
        digit = sb("digit", [P, CAND + 1], I32)
        digs = sb("digs", [P, ROUNDS, CAND + 1], I32)
        steps = sb("steps", [P, ROUNDS, CAND], I32)
        cand = sb("cand", [P, E, CAND], I32)
        fold = sb("fold", [P, E, CAND], I32)
        candf = sb("candf", [P, E, CAND], I32)
        reach = sb("reach", [P, E, CAND], I32)
        dbits = sb("dbits", [P, E], I32)
        above = sb("above", [P, E, NT], BF16)
        tie = sb("tie", [P, E, NT], BF16)
        kept = sb("kept", [P, E, NT], BF16)
        tot = sb("tot", [P, E, NT])
        cum = sb("cum", [P, E, NT])
        rank = sb("rank", [P, E, NT])
        room = sb("room", [P, E])
        nofirst = sb("nofirst", [P, E, NT])
        slot = sb("slot", [P, E, NT], I32)
        slo = sb("slo", [P, E, NT], BF16)
        slf = sb("slf", [P, E, NT], I32)
        slg = sb("slg", [P, E, NT])
        iota_s = sb("iota_s", [P, P, NT], BF16)
        row_i = sb("row_i", [P, 1], I32)
        row_f = sb("row_f", [P, 1])
        tile_i = sb("tile_i", [P, NT], I32)
        tile_f = sb("tile_f", [P, NT])
        vals = sb("vals", [P, E, NT, NV])
        ing = sb("ing", [P, E, NT])
        wrest = sb("wrest", [P, E, NT])
        wpart = sb("wpart", [P, E, NT], BF16)
        slots = sb("slots", [P, E, GE, NV])
        tokf = sb("tokf", [P, E * GE])
        tok = sb("tok", [P, E * GE], I32)
        wslot = sb("wslot", [P, E * GE])
        kvsum = sb("kvsum", [P, 1])
        ssq = sb("ssq", [P, TT])
        bnx = sb("bnx", [P, TT, 6])
        mvx = sb("mvx", [P, TT, 2])
        vq = sb("vq", [P, TT])
        vs = sb("vs", [P, TT])
        rs = sb("rs", [P, TT])
        mhalf = sb("mhalf", [P, TT])
        nmax = sb("nmax", [P, TT])
        esum = sb("esum", [P, TT])
        coef = sb("coef", [P, TT])
        bnh = sb("bnh", [P, TT, 6])
        mvh = sb("mvh", [P, TT, 2])
        vh = sb("vh", [P, TT])
        rh = sb("rh", [P, TT])

        with ExitStack() as early:
            h = alloc(early, "h", [P, TT, D])
            xb = alloc(early, "xb", [P, TT, D])
            prob = alloc(early, "prob", [P, TT, S])
            ctxb = alloc(early, "ctxb", [P, TT, C])
            gamma_b = alloc(early, "gamma_b", [P, S])
            beta_b = alloc(early, "beta_b", [P, S])
            ctxT = alloc(early, "ctxT", [P, S])
            kvT = alloc(early, "kvT", [P, S])
            kvcT = alloc(early, "kvcT", [P, S])
            kvc = alloc(early, "kvc", [P, TT, C])
            xT = alloc(early, "xT", [P, TT, S])
            outT = alloc(early, "outT", [P, S])
            Wk_rows = alloc(early, "Wk_rows", [P, C])
            gw_raw = alloc(early, "gw_raw", [P, KD, P])
            gw = pair(early, "gw", [P, KD, P])
            zT = alloc(early, "zT", [P, S])
        with ExitStack() as late:
            w1r.append(pair(late, "w1r1", [P, KD, 2 * F]))
            w2r.append(pair(late, "w2r1", [P, 2, D]))
            xg = [alloc(late, f"xg{i}", [P, GE, D]) for i in range(2)]
            yr = [alloc(late, f"yr{i}", [P, GE, D]) for i in range(2)]
            hgT = pair(late, "hgT", [P, KD, CAP])
        with ExitStack() as between:
            hot = alloc(between, "hot", [P, 2, P, NT], BF16)
            place = alloc(between, "place", [P, E, NT, GE * NV], BF16)
            hit = alloc(between, "hit", [P, E, CAND, NT], BF16)

        block = stack.enter_context(nc.Block())

        ld_wk, ld_rows, ld_ctx, ld_xb, ld_w1, ld_w2 = (sem(n) for n in
            ("ld_wk", "ld_rows", "ld_ctx", "ld_xb", "ld_w1", "ld_w2"))
        ld_x = [sem(f"ld_x{i}") for i in range(NB)]
        st_h = sem("st_h")
        st_out = sem("st_out")
        gath = [sem(f"gath{i}") for i in range(2)]
        scat = [sem(f"scat{i}") for i in range(2)]
        y_landed = sem("y_landed")
        c_pool, c_iota, c_wk, c_wkT, c_tanh, c_gw = (sem(n) for n in ("c_pool", "c_iota", "c_wk", "c_wkT", "c_tanh", "c_gw"))
        w1_hi, w1_lo, w2_hi, w2_lo = (sem(n) for n in ("w1_hi", "w1_lo", "w2_hi", "w2_lo"))
        p_ctxT, p_xT, p_kvT, p_kvc, p_outT, p_S = (sem(n) for n in
            ("p_ctxT", "p_xT", "p_kvT", "p_kvc", "p_outT", "p_S"))
        e_ctxT, e_xT, e_kvT, e_kvcT, e_kvc, e_outT = (sem(n) for n in
            ("e_ctxT", "e_xT", "e_kvT", "e_kvcT", "e_kvc", "e_outT"))
        e_ssq, e_vs, e_rs, e_scaled, e_logit, e_exp, e_vh, e_rh, e_h = (sem(n) for n in
            ("e_ssq", "e_vs", "e_rs", "e_scaled", "e_logit", "e_exp", "e_vh", "e_rh", "e_h"))
        p_hT, p_zT, p_z, p_x2, p_x1, p_y = (sem(n) for n in ("p_hT", "p_zT", "p_z", "p_x2", "p_x1", "p_y"))
        e_hi, e_hT, e_zT, e_z, e_th, e_u, e_g, e_ghi, e_glo, e_y = (sem(n) for n in
            ("e_hi", "e_hT", "e_zT", "e_z", "e_th", "e_u", "e_g", "e_ghi", "e_glo", "e_y"))
        r_sig, r_hit, r_cnt, r_tie, r_tieP, r_kept, r_keptP, r_hot, r_slot, r_idx = (sem(n) for n in
            ("r_sig", "r_hit", "r_cnt", "r_tie", "r_tieP", "r_kept", "r_keptP", "r_hot", "r_slot", "r_idx"))
        q_hgT, q_x2, q_x1, q_y = (sem(n) for n in ("q_hgT", "q_x2", "q_x1", "q_y"))
        f_hi, f_hgT, f_th, f_g, f_ghi, f_glo, f_y = (sem(n) for n in
            ("f_hi", "f_hgT", "f_th", "f_g", "f_ghi", "f_glo", "f_y"))

        def bc(ap, shape):
            return ap.broadcast_to(shape)

        counts = bank[7][:, 0:E * CAND]
        zps = bank[7][:, :].rearrange("p (t e) -> p t e", e=P)
        prefix_ps = bank[7][:, 128:128 + E * NT]
        total_ps = bank[7][:, 256:256 + E * NT]
        slots_ps = bank[7][:, 384:384 + E * GE * NV]
        above_ps = bank[0][:, 0:E * NT]

        HT_BANK = (4, 6, 5, 4)
        X2_BANK, X1_BANK = (5, 6), (4, 5)
        Y_BANK = (6, 4, 5, 6)

        @block.sync
        def _(sp):
            def row(v, n):
                return v.rearrange("(o n) -> o n", o=1).broadcast_to([P, n])

            sp.dma_start(ctxb[:, :, :], ctx_in[0].rearrange("(t p) c -> p t c", p=P)).then_inc(ld_ctx, 16)
            sp.dma_start(Wk_rows[:, :], W_k).then_inc(ld_wk, 16)
            sp.dma_start(xb[:, :, :], x[0].rearrange("(t p) d -> p t d", p=P)).then_inc(ld_xb, 16)
            sp.dma_start(bk_col[:, :], b_k.rearrange("(p o) -> p o", o=1)).then_inc(ld_wk, 16)
            sp.dma_start(xs[:, 0:TT, :], x[0].rearrange("(t p) d -> p t d", p=P)).then_inc(ld_x[0], 16)
            sp.dma_start(gamma_b[:, :], row(gamma, S)).then_inc(ld_rows, 16)
            sp.dma_start(beta_b[:, :], row(beta, S)).then_inc(ld_rows, 16)
            sp.dma_start(gates[:, 0:1], row(g_x, 1)).then_inc(ld_rows, 16)
            sp.dma_start(gates[:, 1:2], row(g_f, 1)).then_inc(ld_rows, 16)
            sp.dma_start(eb[:, :], row(ebias, E)).then_inc(ld_rows, 16)
            sp.wait_ge(c_gw, 1)
            sp.dma_start(gw_raw[:, :, 0:E], gate_w.rearrange("(k p) e -> p k e", p=P)).then_inc(ld_rows, 16)
            sp.dma_start(w1_raw[:, :, :], sw1[0].rearrange("(k p) f -> p k f", p=P)).then_inc(ld_w1, 16)
            sp.dma_start(w2_raw[:, :, :], sw2[0].rearrange("(k p) d -> p k d", p=P)).then_inc(ld_w2, 16)
            for b in range(1, NB):
                sp.dma_start(xs[:, b * TT:(b + 1) * TT, :], x[b].rearrange("(t p) d -> p t d", p=P)).then_inc(ld_x[b], 16)
            h_rows = h_dram.rearrange("(b t p) d -> b p t d", p=P, t=TT)
            out_rows = out.rearrange("b (t p) d -> b p t d", p=P)
            ctx_rows = ctx_in.rearrange("b (t p) c -> b p t c", p=P)
            x_rows = x.rearrange("b (t p) d -> b p t d", p=P)
            with sp.Fori(0, NB - 1) as b:
                sp.wait_ge(p_ctxT, b + 1)
                sp.dma_start(ctxb[:, :, :], ctx_rows[bass.ds(b + 1, 1), :, :, :].rearrange("o p t c -> (o p) t c")).then_inc(ld_ctx, 16)
                sp.wait_ge(p_xT, TT * b + TT)
                sp.dma_start(xb[:, :, :], x_rows[bass.ds(b + 1, 1), :, :, :].rearrange("o p t d -> (o p) t d")).then_inc(ld_xb, 16)
                sp.wait_ge(e_h, b + 1)
                sp.dma_start(h_rows[bass.ds(b, 1), :, :, :].rearrange("o p t d -> (o p) t d"), h[:, :, :]).then_inc(st_h, 16)
            sp.wait_ge(w1_lo, W1N)
            sp.wait_ge(w2_lo, W2N)
            sp.dma_start(w1_raw[:, :, :], rw1[0].rearrange("(k p) f -> p k f", p=P)).then_inc(ld_w1, 16)
            sp.dma_start(w2_raw[:, :, :], rw2[0].rearrange("(k p) d -> p k d", p=P)).then_inc(ld_w2, 16)
            sp.wait_ge(e_h, NB)
            sp.dma_start(h_rows[NB - 1], h[:, :, :]).then_inc(st_h, 16)
            with sp.Fori(0, NB) as b:
                sp.wait_ge(e_y, TT * b + 2 * TT)
                sp.dma_start(out_rows[bass.ds(b, 1), :, :, :].rearrange("o p t d -> (o p) t d"),
                             xs[:, bass.ds(b * TT, TT), :]).then_inc(st_out, 16)
            w1_rows = rw1.rearrange("e (k p) f -> e p k f", p=P)
            w2_rows = rw2.rearrange("e (k p) d -> e p k d", p=P)
            with sp.Fori(1, E) as e:
                sp.wait_ge(w1_lo, W1N * e + W1N)
                sp.dma_start(w1_raw[:, :, :], w1_rows[bass.ds(e, 1), :, :, :].rearrange("o p k f -> (o p) k f")).then_inc(ld_w1, 16)
                sp.wait_ge(w2_lo, W2N * e + W2N)
                sp.dma_start(w2_raw[:, :, :], w2_rows[bass.ds(e, 1), :, :, :].rearrange("o p k d -> (o p) k d")).then_inc(ld_w2, 16)

        @block.tensor
        def _(pe):
            def transpose(out_ap, in_ap, n=P):
                return nc.tensor.transpose(out_ap, in_ap, ident[0:n, 0:n])

            def product(out_ap, pieces):
                todo = [(w[i], m[j]) for w, m in pieces for i, j in ((0, 0), (0, 1), (1, 0))]
                for n, (w, m) in enumerate(todo):
                    last = nc.tensor.matmul(out_ap, w, m, start=n == 0, stop=n == len(todo) - 1)
                return last

            def both(p, *at):
                return p[0][at], p[1][at]

            A = slice(None)

            def context(b):
                pe.wait_ge(ld_ctx, 16 * b + 16)
                if not isinstance(b, int) or b > 0:
                    pe.wait_ge(e_scaled, TT * b - 3)
                for t in range(TT):
                    last = transpose(bank[0][:, t * P:(t + 1) * P], ctxb[:, t, :])
                last.then_inc(p_ctxT, 1)

            def x_cols(b, j, bk):
                for t in range(TT):
                    last = transpose(bank[bk][:, t * P:(t + 1) * P], xb[:, t, j * P:(j + 1) * P])
                last.then_inc(p_xT, 1)

            def keys(b):
                later = not isinstance(b, int) or b > 0
                pe.wait_ge(ld_xb, 16 * b + 16)
                if later:
                    pe.wait_ge(e_scaled, TT * b - 2)
                x_cols(b, 0, 1)
                pe.wait_ge(e_ctxT, b + 1)
                if later:
                    pe.wait_ge(e_scaled, TT * b - 1)
                nc.tensor.matmul(bank[2][:, :], WkT[:, :], ctxT[:, :], start=True, stop=True).then_inc(p_kvT, 1)

            def more_x(b):
                if not isinstance(b, int) or b > 0:
                    pe.wait_ge(e_scaled, TT * b)
                x_cols(b, 1, 3)
                x_cols(b, 2, 0)

            def keys_back(b):
                pe.wait_ge(e_kvcT, b + 1)
                pe.wait_ge(e_xT, TT * b + 1)
                for t in range(TT):
                    last = transpose(bank[1][:, t * C:(t + 1) * C], kvcT[:, t * P:(t + 1) * P])
                last.then_inc(p_kvc, 1)
                x_cols(b, 3, 2)

            def attend(b):
                pe.wait_ge(e_kvc, b + 1)
                for j in range(TT):
                    if j != 1:
                        pe.wait_ge(e_xT, TT * b + max(j, 1) + 1)
                    last = nc.tensor.matmul(bank[3][:, :], kvc[:, j, :], xT[:, j, :], start=j == 0, stop=j == TT - 1)
                last.then_inc(p_outT, 1)

            def scores(b):
                pe.wait_ge(e_outT, b + 1)
                for t in range(TT):
                    nc.tensor.matmul(bank[t][:, :], outT[:, t * P:(t + 1) * P], kvcT[:, :], start=True, stop=True).then_inc(p_S, 1)

            def rows_back(f):
                later = not isinstance(f, int) or f > 0
                pe.wait_ge(e_h, f + 1)
                for k in range(KD):
                    if later and k == 0:
                        pe.wait_ge(e_g, 2 * f - 1)
                    if later and k == 1:
                        pe.wait_ge(e_u, 2 * f)
                    if later and k == 2:
                        pe.wait_ge(e_g, 2 * f)
                    if k == 3:
                        pe.wait_ge(e_hT, KD * f + 1)
                    for t in range(TT):
                        last = transpose(bank[HT_BANK[k]][:, t * P:(t + 1) * P], h[:, t, k * P:(k + 1) * P])
                    last.then_inc(p_hT, 1)
                pe.wait_ge(e_hT, KD * f + KD)
                pe.wait_ge(e_z, f + 1)
                product(bank[7][:, :], [(both(gw, A, k, A), both(hT, A, k, A)) for k in range(KD)]).then_inc(p_zT, 1)

            def logits(f):
                pe.wait_ge(e_zT, f + 1)
                for t in range(TT):
                    last = transpose(zps[:, t, :], zT[:, t * P:(t + 1) * P])
                last.then_inc(p_z, 1)

            def up(f):
                for half in range(2):
                    pe.wait_ge(e_y, TT * f + 3 + half)
                    for w_col, bk, done in ((F, X2_BANK[half], p_x2), (0, X1_BANK[half], p_x1)):
                        if half == 1 and done is p_x1:
                            pe.wait_ge(e_u, 2 * f + 1)
                        col = slice(w_col + half * P, w_col + half * P + P)
                        product(bank[bk][:, :], [(both(w1s, A, k, col), both(hT, A, k, A)) for k in range(KD)]).then_inc(done, 1)

            def down(f, t):
                pe.wait_ge(e_glo, 2 * f + 2)
                if t == 3:
                    pe.wait_ge(e_y, TT * f + TT + 1)
                col = slice(t * P, (t + 1) * P)
                product(bank[Y_BANK[t]][:, :], [(both(gT, A, k, col), both(w2s, A, k, A)) for k in range(2)]).then_inc(p_y, 1)

            pe.wait_ge(c_pool, 4)
            pe.wait_ge(ld_wk, 32)
            transpose(bank[7][:, 0:C], Wk_rows[:, :]).then_inc(c_wk, 1)
            context(0)
            pe.wait_ge(c_wkT, 1)
            for b in range(2):
                if b == 1:
                    context(1)
                keys(b)
                more_x(b)
                keys_back(b)
                attend(b)
                if b == 0:
                    scores(0)
            pe.wait_ge(c_gw, 3)
            pe.wait_ge(w1_lo, W1N)
            pe.wait_ge(w2_lo, W2N)
            scores(1)
            rows_back(0)
            logits(0)
            with pe.Fori(2, NB) as b:
                up(b - 2)
                rows_back(b - 1)
                context(b)
                keys(b)
                down(b - 2, 0)
                logits(b - 1)
                more_x(b)
                down(b - 2, 1)
                keys_back(b)
                down(b - 2, 2)
                attend(b)
                down(b - 2, 3)
                scores(b)
            up(NB - 2)
            rows_back(NB - 1)
            down(NB - 2, 0)
            logits(NB - 1)
            for t in range(1, TT):
                down(NB - 2, t)
            up(NB - 1)
            for t in range(TT):
                down(NB - 1, t)

            with pe.Fori(0, ROUNDS) as r:
                pe.wait_ge(r_hit, r + 1)
                for t in range(NT):
                    last = nc.tensor.matmul(counts, ones[:, :], hit[:, :, :, t], start=t == 0, stop=t == NT - 1)
                last.then_inc(r_cnt, 1)
            for given, flags, done in ((r_tie, tie, r_tieP), (r_kept, kept, r_keptP)):
                pe.wait_ge(given, 1)
                flat = flags[:, :, :].rearrange("p e t -> p (e t)")
                if flags is tie:
                    nc.tensor.matmul(above_ps, ones[:, :], above[:, :, :].rearrange("p e t -> p (e t)"), start=True, stop=True)
                nc.tensor.matmul(prefix_ps, lower[:, :], flat, start=True, stop=True)
                nc.tensor.matmul(total_ps, ones[:, :], flat, start=True, stop=True).then_inc(done, 1)
            for e in range(E):
                pe.wait_ge(r_hot, e + 1)
                for t in range(NT):
                    last = nc.tensor.matmul(slots_ps[:, e * GE * NV:(e + 1) * GE * NV], hot[:, e % 2, :, t], place[:, e, t, :],
                                            start=t == 0, stop=t == NT - 1)
                last.then_inc(r_slot, 1)

            def gathered(e, par):
                pe.wait_ge(gath[par], (e - par) * (8 * GE) + 16 * GE)
                for k in range(KD):
                    if not isinstance(e, int) or e > 0:
                        pe.wait_ge(f_hgT, KD * e - KD + k + 1)
                    for g in range(GE):
                        last = transpose(bank[k][:, g * P:g * P + GSZ[g]], xg[par][0:GSZ[g], g, k * P:(k + 1) * P], GSZ[g])
                    last.then_inc(q_hgT, 1)

            def routed_up(e, par):
                pe.wait_ge(f_hgT, KD * e + KD)
                pe.wait_ge(w1_lo, W1N * e + 2 * W1N)
                for half in range(2):
                    for part, (w_col, done) in enumerate(((F, q_x2), (0, q_x1))):
                        bk = 2 * half + part
                        if not isinstance(e, int) or e > 0:
                            pe.wait_ge(f_y, GE * e - GE + bk + 1) if bk < GE else pe.wait_ge(f_g, 2 * e)
                        col = slice(w_col + half * P, w_col + half * P + P)
                        product(bank[4 + bk][:, 0:CAP], [(both(w1r[par], A, k, col), both(hgT, A, k, A)) for k in range(KD)]).then_inc(done, 1)

            def routed_down(e, par):
                pe.wait_ge(f_glo, 2 * e + 2)
                pe.wait_ge(w2_lo, W2N * e + 2 * W2N)
                for g in range(GE):
                    col = slice(g * P, g * P + GSZ[g])
                    product(bank[4 + g][0:GSZ[g], :], [(both(gT, A, k, col), both(w2r[par], A, k, A)) for k in range(2)]).then_inc(q_y, 1)

            pe.wait_ge(e_y, TT * NB + TT)
            gathered(0, 0)
            routed_up(0, 0)
            with pe.Fori(1, E, 2) as e:
                gathered(e, 1)
                routed_down(e - 1, 0)
                routed_up(e, 1)
                gathered(e + 1, 0)
                routed_down(e, 1)
                routed_up(e + 1, 0)
            routed_down(E - 1, 0)

        @block.scalar
        def _(act):
            def copy(dst, src):
                return nc.scalar.activation(dst, src, ACT.Copy)

            def upper_w1(n, w1, k):
                if k == 0:
                    act.wait_ge(ld_w1, 16 * n + 16)
                copy(w1[0][:, k, :], w1_raw[:, k, :]).then_inc(w1_hi, 1)

            def upper_w2(n, w2, k):
                if k == 0:
                    act.wait_ge(ld_w2, 16 * n + 16)
                copy(w2[0][:, k, :], w2_raw[:, k, :]).then_inc(w2_hi, 1)

            def upper_weights(n, w1, w2):
                for k in range(W1N):
                    upper_w1(n, w1, k)
                for k in range(W2N):
                    upper_w2(n, w2, k)

            def x_copy(b, j, bk):
                act.wait_ge(p_xT, TT * b + j + 1)
                copy(xT[:, j, :], bank[bk][:, :]).then_inc(e_xT, 1)

            def front(b):
                act.wait_ge(p_ctxT, b + 1)
                copy(ctxT[:, :], bank[0][:, :]).then_inc(e_ctxT, 1)
                x_copy(b, 0, 1)
                act.wait_ge(p_kvT, b + 1)
                nc.scalar.activation(kvT[:, :], bank[2][:, :], ACT.Identity, bias=bk_col[:, 0:1],
                                     accum_out=kvsum[:, :]).then_inc(e_kvT, 1)
                x_copy(b, 1, 3)
                x_copy(b, 2, 0)
                act.wait_ge(p_kvc, b + 1)
                copy(kvc[:, :, :].rearrange("p t c -> p (t c)"), bank[1][:, :]).then_inc(e_kvc, 1)
                x_copy(b, 3, 2)
                act.wait_ge(p_outT, b + 1)
                copy(outT[:, :], bank[3][:, :]).then_inc(e_outT, 1)

            def squares(b):
                if not isinstance(b, int) or b > 0:
                    act.wait_ge(e_h, b)
                for t in range(TT):
                    act.wait_ge(p_S, TT * b + t + 1)
                    nc.scalar.activation(prob[:, t, :], bank[t][:, :], ACT.Square, accum_out=ssq[:, t:t + 1]).then_inc(e_ssq, 1)

            def exps(b):
                for t in range(TT):
                    act.wait_ge(e_logit, TT * b + t + 1)
                    nc.scalar.activation(prob[:, t, :], prob[:, t, :], ACT.Exp, bias=nmax[:, t:t + 1], scale=-1.0,
                                         accum_out=esum[:, t:t + 1]).then_inc(e_exp, 1)

            def rows_upper(f):
                for k in range(KD):
                    act.wait_ge(p_hT, KD * f + k + 1)
                    copy(hT[0][:, k, :], bank[HT_BANK[k]][:, :]).then_inc(e_hi, 1)
                act.wait_ge(p_zT, f + 1)
                copy(zT[:, :], bank[7][:, :]).then_inc(e_zT, 1)

            def gate_tanh(f, half):
                act.wait_ge(p_x2, 2 * f + half + 1)
                nc.scalar.activation(th[:, half, :], bank[X2_BANK[half]][:, :], ACT.Tanh, scale=0.5).then_inc(e_th, 1)

            def gate_upper(f, half):
                act.wait_ge(e_g, 2 * f + half + 1)
                copy(gT[0][:, half, :], gf[:, half, :]).then_inc(e_ghi, 1)

            act.wait_ge(c_wk, 1)
            copy(WkT[:, :], bank[7][:, 0:C]).then_inc(c_wkT, 1)
            front(0)
            act.wait_ge(ld_rows, 16 * 6)
            nc.scalar.activation(gt[:, :], gates[:, :], ACT.Tanh).then_inc(c_tanh, 1)
            squares(0)
            copy(gw[0][:, :, :], gw_raw[:, :, :]).then_inc(c_gw, 1)
            upper_weights(0, w1s, w2s)
            exps(0)
            front(1)
            squares(1)
            rows_upper(0)
            with act.Fori(2, NB) as b:
                gate_tanh(b - 2, 0)
                exps(b - 1)
                gate_upper(b - 2, 0)
                gate_tanh(b - 2, 1)
                gate_upper(b - 2, 1)
                rows_upper(b - 1)
                front(b)
                squares(b)
            gate_tanh(NB - 2, 0)
            exps(NB - 1)
            gate_upper(NB - 2, 0)
            gate_tanh(NB - 2, 1)
            gate_upper(NB - 2, 1)
            rows_upper(NB - 1)
            gate_tanh(NB - 1, 0)
            gate_upper(NB - 1, 0)
            gate_tanh(NB - 1, 1)
            gate_upper(NB - 1, 1)
            act.wait_ge(e_z, NB + 1)
            nc.scalar.activation(wt[:, :, :].rearrange("p e t -> p (e t)"), z[:, :, :].rearrange("p e t -> p (e t)"),
                                 ACT.Tanh, scale=0.5).then_inc(r_sig, 1)
            upper_weights(1, w1r[0], w2r[0])

            def gathered_upper(e):
                for k in range(KD):
                    act.wait_ge(q_hgT, KD * e + k + 1)
                    copy(hgT[0][:, k, :], bank[k][:, 0:CAP]).then_inc(f_hi, 1)

            def routed_tanh(e, half):
                act.wait_ge(q_x2, 2 * e + half + 1)
                nc.scalar.activation(th[:, half, 0:CAP], bank[4 + 2 * half][:, 0:CAP], ACT.Tanh, scale=0.5).then_inc(f_th, 1)

            def routed_gate_upper(e, half):
                act.wait_ge(f_g, 2 * e + half + 1)
                copy(gT[0][:, half, 0:CAP], gf[:, half, 0:CAP]).then_inc(f_ghi, 1)

            def scaled(e, par, g):
                if g == 0:
                    act.wait_ge(y_landed, e + 1)
                act.wait_ge(q_y, GE * e + g + 1)
                w = wslot[0:GSZ[g], e * GE + g:e * GE + g + 1] if isinstance(e, int) else wslot[0:GSZ[g], bass.ds(e * GE + g, 1)]
                nc.scalar.activation(yr[par][0:GSZ[g], g, :], bank[4 + g][0:GSZ[g], :], ACT.Copy, scale=w).then_inc(f_y, 1)

            def expert(e, par):
                first, last = isinstance(e, int) and e == 0, isinstance(e, int) and e == E - 1
                w1, w2 = w1r[1 - par], w2r[1 - par]
                gathered_upper(e)
                for g in range(GE):
                    if not last:
                        upper_w1(e + 2, w1, g)
                    if not first:
                        scaled(e - 1, 1 - par, g)
                routed_tanh(e, 0)
                if not last:
                    upper_w1(e + 2, w1, KD - 1)
                routed_gate_upper(e, 0)
                routed_tanh(e, 1)
                if not last:
                    upper_w2(e + 2, w2, 0)
                    upper_w2(e + 2, w2, 1)
                routed_gate_upper(e, 1)

            act.wait_ge(r_idx, 1)
            expert(0, 0)

            with act.Fori(1, E - 2, 2) as e:
                expert(e, 1)
                expert(e + 1, 0)
            expert(E - 2, 1)
            expert(E - 1, 0)
            for g in range(GE):
                scaled(E - 1, 0, g)

        @block.gpsimd
        def _(pool):
            g_ = nc.gpsimd
            g_.memset(ident[:, :], 0.0)
            g_.memset(ones[:, :], 1.0).then_inc(c_pool, 1)
            g_.memset(mhalf[:, :], -0.5).then_inc(c_pool, 1)
            g_.memset(gw_raw[:, :, :], 0.0).then_inc(c_gw, 1)
            g_.drain()
            g_.affine_select(out=ident[:, :], in_=ident[:, :], compare_op=ALU.not_equal, fill=1.0, base=0,
                             pattern=[[-1, P]], channel_multiplier=1).then_inc(c_pool, 1)
            g_.affine_select(out=lower[:, :], in_=ones[:, :], compare_op=ALU.is_gt, fill=0.0, base=0,
                             pattern=[[1, P]], channel_multiplier=-1).then_inc(c_pool, 1)
            g_.iota(prefi[:, :, 0], [[-1, E]], base=E, channel_multiplier=0).then_inc(c_iota, 1)
            g_.iota(row_i[:, :], [[0, 1]], base=0, channel_multiplier=1).then_inc(c_iota, 1)
            g_.iota(tile_i[:, :], [[1, NT]], base=0, channel_multiplier=0).then_inc(c_iota, 1)
            g_.iota(digit[:, :], [[1, CAND + 1]], base=0, channel_multiplier=0).then_inc(c_iota, 1)
            g_.iota(iota_s[:, :, :], [[1, P], [0, NT]], base=0, channel_multiplier=0,
                    allow_small_or_imprecise_dtypes=True).then_inc(c_iota, 1)

            def inverse_root_scores(b):
                pool.wait_ge(e_vs, b + 1)
                g_.tensor_tensor(rs[:, :], vs[:, :], mhalf[:, :], ALU.pow).then_inc(e_rs, 1)

            def inverse_root_rows(b):
                pool.wait_ge(e_vh, b + 1)
                g_.tensor_tensor(rh[:, :], vh[:, :], mhalf[:, :], ALU.pow).then_inc(e_rh, 1)

            def lower_weights(n, w1, w2):
                for w, raw, pieces, hi, lo in ((w1, w1_raw, W1N, w1_hi, w1_lo), (w2, w2_raw, W2N, w2_hi, w2_lo)):
                    for k in range(pieces):
                        pool.wait_ge(hi, pieces * n + k + 1)
                        g_.tensor_tensor(w[1][:, k, :], raw[:, k, :], w[0][:, k, :].bitcast(F32), ALU.subtract).then_inc(lo, 1)

            inverse_root_scores(0)
            lower_weights(0, w1s, w2s)
            inverse_root_rows(0)
            with pool.Fori(1, NB) as b:
                inverse_root_scores(b)
                inverse_root_rows(b)
            lower_weights(1, w1r[0], w2r[0])

            pool.wait_ge(st_h, 16 * NB)
            pool.wait_ge(r_idx, 1)

            def index(e, g):
                return bass.IndirectOffsetOnAxis(ap=tok[0:GSZ[g], e * GE + g:e * GE + g + 1].bitcast(U32), axis=0)

            def gather(e):
                for g in range(GE):
                    g_.indirect_dma_start(xg[e % 2][0:GSZ[g], g, :], None, h_dram, index(e, g),
                                          bounds_check=T - 1).then_inc(gath[e % 2], 16)

            rows = out.rearrange("b s d -> (b s) d")
            g_.sem_inc(y_landed, 2)
            gather(0)
            gather(1)
            pool.wait_ge(st_out, 16 * NB)
            for e in range(E):
                if e + 2 < E:
                    pool.wait_ge(q_hgT, KD * e + KD)
                    gather(e + 2)
                if e >= 1:
                    pool.wait_ge(scat[(e - 1) % 2], 16 * GE * ((e - 1) // 2 + 1))
                    g_.sem_inc(y_landed, 1)
                pool.wait_ge(f_y, GE * (e + 1))
                for g in range(GE):
                    g_.indirect_dma_start(rows, index(e, g), yr[e % 2][0:GSZ[g], g, :], None, bounds_check=T - 1,
                                          compute_op=ALU.add).then_inc(scat[e % 2], 16)
            for i in range(2):
                pool.wait_ge(scat[i], 16 * GE * len(range(i, E, 2)))

        @block.vector
        def _(dve):
            v = nc.vector

            def settle():
                return v.drain()

            v.sem_inc(e_y, TT)
            v.sem_inc(e_z, 1)

            def tile_of(t):
                return xs[:, t, :] if isinstance(t, int) else xs[:, bass.ds(t, 1), :].rearrange("p o d -> p (o d)")

            def x_stats(b):
                for t in range(TT):
                    v.bn_stats(bnx[:, t, :], tile_of(b * TT + t))
                settle()
                for t in range(TT):
                    v.bn_aggr(mvx[:, t, :], bnx[:, t, :])
                settle()
                v.tensor_scalar(vq[:, :], mvx[:, :, 1], EPS_LN, EPS_SIM * SIM_SCALE2, ALU.add, ALU.mult)

            def centre_keys(b):
                dve.wait_ge(e_kvT, b + 1)
                v.tensor_scalar(kvsum[:, :], kvsum[:, :], 1.0 / S, None, ALU.mult)
                settle()
                v.tensor_scalar(kvcT[:, :], kvT[:, :], kvsum[:, 0:1], None, ALU.subtract).then_inc(e_kvcT, 1)

            def score_variance(b):
                dve.wait_ge(e_ssq, TT * b + TT)
                v.scalar_tensor_tensor(vs[:, :], ssq[:, :], 1.0 / S, vq[:, :], ALU.mult, ALU.add).then_inc(e_vs, 1)

            def softmax_inputs(b):
                dve.wait_ge(e_rs, b + 1)
                for t in range(TT):
                    v.scalar_tensor_tensor(prob[:, t, :], bank[t][:, :], rs[:, t:t + 1], gamma_b[:, :],
                                           ALU.mult, ALU.mult).then_inc(e_scaled, 1)
                settle()
                for t in range(TT):
                    v.tensor_tensor_reduce(out=prob[:, t, :], in0=prob[:, t, :], in1=beta_b[:, :], scale=-1.0,
                                           scalar=3.0e38, op0=ALU.add, op1=ALU.min,
                                           accum_out=nmax[:, t:t + 1]).then_inc(e_logit, 1)

            def add_attention(b):
                dve.wait_ge(e_exp, TT * b + TT)
                v.reciprocal(coef[:, :], esum[:, :])
                settle()
                v.tensor_scalar(coef[:, :], coef[:, :], gt[:, 0:1], None, ALU.mult)
                settle()
                for t in range(TT):
                    v.scalar_tensor_tensor(tile_of(b * TT + t), prob[:, t, :], coef[:, t:t + 1], tile_of(b * TT + t),
                                           ALU.mult, ALU.add)
                settle()

            def row_stats(b):
                for t in range(TT):
                    v.bn_stats(bnh[:, t, :], tile_of(b * TT + t))
                settle()
                for t in range(TT):
                    v.bn_aggr(mvh[:, t, :], bnh[:, t, :])
                settle()
                v.tensor_scalar(vh[:, :], mvh[:, :, 1], EPS_LN, None, ALU.add).then_inc(e_vh, 1)

            def normalise(b):
                dve.wait_ge(e_rh, b + 1)
                if not isinstance(b, int) or b > 0:
                    dve.wait_ge(p_hT, KD * b)
                    dve.wait_ge(st_h, 16 * b)
                for t in range(TT):
                    last = v.tensor_scalar(h[:, t, :], tile_of(b * TT + t), mvh[:, t, 0:1], rh[:, t:t + 1],
                                           ALU.subtract, ALU.mult)
                last.then_inc(e_h, 1)

            def rows_lower(f):
                for k in range(KD):
                    dve.wait_ge(e_hi, KD * f + k + 1)
                    v.tensor_tensor(hT[1][:, k, :], bank[HT_BANK[k]][:, :], hT[0][:, k, :].bitcast(F32), ALU.subtract).then_inc(e_hT, 1)

            def take_logits(f):
                dve.wait_ge(p_z, f + 1)
                zt = z[:, :, f * TT:(f + 1) * TT] if isinstance(f, int) else z[:, :, bass.ds(f * TT, TT)]
                v.tensor_tensor(zt.rearrange("p e t -> p t e"), zps[:, :, 0:E], bc(eb[:, :].unsqueeze(1), [P, TT, E]), ALU.add).then_inc(e_z, 1)

            def gate(f, half):
                dve.wait_ge(e_th, 2 * f + half + 1)
                v.scalar_tensor_tensor(th[:, half, :], th[:, half, :], 1.0, bank[X2_BANK[half]][:, :], ALU.add, ALU.mult).then_inc(e_u, 1)
                settle()
                dve.wait_ge(p_x1, 2 * f + half + 1)
                v.scalar_tensor_tensor(gf[:, half, :], th[:, half, :], 0.5, bank[X1_BANK[half]][:, :], ALU.mult, ALU.mult).then_inc(e_g, 1)

            def gate_lower(f, half):
                dve.wait_ge(e_ghi, 2 * f + half + 1)
                v.tensor_tensor(gT[1][:, half, :], gf[:, half, :], gT[0][:, half, :].bitcast(F32), ALU.subtract).then_inc(e_glo, 1)

            def add_shared(f, t):
                dve.wait_ge(p_y, TT * f + t + 1)
                v.scalar_tensor_tensor(tile_of(f * TT + t), bank[Y_BANK[t]][:, :], gt[:, 1:2], tile_of(f * TT + t),
                                       ALU.mult, ALU.add).then_inc(e_y, 1)

            dve.wait_ge(ld_x[0], 16)
            x_stats(0)
            centre_keys(0)
            dve.wait_ge(c_iota, 5)
            v.tensor_copy(pref[:, :, :], prefi[:, :, :])
            v.tensor_copy(row_f[:, :], row_i[:, :])
            v.tensor_copy(tile_f[:, :], tile_i[:, :])
            v.memset(nofirst[:, :, :], 1.0)
            v.memset(thr[:, :], -2 ** 31)
            for r in range(ROUNDS):
                v.tensor_scalar(digs[:, r, :], digit[:, :], 32 - DIGIT * (r + 1), None, ALU.logical_shift_left)
            settle()
            v.memset(nofirst[:, :, 0:1], 0.0)
            v.tensor_tensor(steps[:, :, :], digs[:, :, 1:], digs[:, :, 0:CAND], ALU.bitwise_xor)
            settle()
            v.tensor_copy(vals[:, :, :, 0], bc(tile_f[:, :].unsqueeze(1), [P, E, NT]))
            v.tensor_copy(vals[:, :, :, 1], bc(row_f[:, :].unsqueeze(2), [P, E, NT]))
            dve.wait_ge(ld_rows, 16 * 6)
            dve.wait_ge(c_tanh, 1)
            score_variance(0)
            softmax_inputs(0)
            dve.wait_ge(c_gw, 2)
            v.tensor_tensor(gw[1][:, :, :], gw_raw[:, :, :], gw[0][:, :, :].bitcast(F32), ALU.subtract).then_inc(c_gw, 1)
            add_attention(0)
            row_stats(0)
            centre_keys(1)
            for b in range(1, NB):
                dve.wait_ge(ld_x[b], 16)
            x_stats(1)
            normalise(0)
            score_variance(1)
            rows_lower(0)
            take_logits(0)
            with dve.Fori(2, NB) as b:
                softmax_inputs(b - 1)
                gate(b - 2, 0)
                add_attention(b - 1)
                row_stats(b - 1)
                gate_lower(b - 2, 0)
                gate(b - 2, 1)
                normalise(b - 1)
                gate_lower(b - 2, 1)
                x_stats(b)
                rows_lower(b - 1)
                add_shared(b - 2, 0)
                centre_keys(b)
                take_logits(b - 1)
                add_shared(b - 2, 1)
                add_shared(b - 2, 2)
                add_shared(b - 2, 3)
                score_variance(b)
            softmax_inputs(NB - 1)
            gate(NB - 2, 0)
            add_attention(NB - 1)
            row_stats(NB - 1)
            gate_lower(NB - 2, 0)
            gate(NB - 2, 1)
            normalise(NB - 1)
            gate_lower(NB - 2, 1)
            rows_lower(NB - 1)
            add_shared(NB - 2, 0)
            take_logits(NB - 1)
            for t in range(1, TT):
                add_shared(NB - 2, t)
            for half in range(2):
                gate(NB - 1, half)
                gate_lower(NB - 1, half)
            for t in range(TT):
                add_shared(NB - 1, t)

            def per_token(ap):
                return bc(ap.unsqueeze(1), [P, E, NT])

            def choose(src, one):
                v.tensor_reduce(m1[:, :], src[:, :, :].rearrange("p e t -> p t e"), AX.X, ALU.max)
                settle()
                v.tensor_tensor(eq[:, :, :], src[:, :, :], per_token(m1[:, :]), ALU.is_equal)
                settle()
                v.tensor_tensor(key[:, :, :], eq[:, :, :], bc(pref[:, :, :], [P, E, NT]), ALU.mult)
                settle()
                v.tensor_reduce(m1[:, :], key[:, :, :].rearrange("p e t -> p t e"), AX.X, ALU.max)
                settle()
                v.tensor_tensor(one[:, :, :], key[:, :, :], per_token(m1[:, :]), ALU.is_equal)
                settle()

            settle()
            choose(z, one1)
            v.scalar_tensor_tensor(z2[:, :, :], one1[:, :, :], -3.0e38, z[:, :, :], ALU.mult, ALU.add)
            settle()
            choose(z2, one2)
            v.tensor_tensor(mask[:, :, :], one1[:, :, :], one2[:, :, :], ALU.add)
            settle()
            v.tensor_tensor(zs[:, :, :], z[:, :, :], mask[:, :, :], ALU.mult)
            v.tensor_scalar(key[:, :, :], mask[:, :, :], -1.0, -UNMASKED, ALU.add, ALU.mult)
            settle()
            v.tensor_tensor(zs[:, :, :], zs[:, :, :], key[:, :, :], ALU.add)
            dve.wait_ge(r_sig, 1)
            v.tensor_scalar(wt[:, :, :], wt[:, :, :], 0.5, 0.5, ALU.mult, ALU.add)
            settle()
            v.scalar_tensor_tensor(wt[:, :, :], wt[:, :, :], gt[:, 1:2], mask[:, :, :], ALU.mult, ALU.mult)
            settle()

            def as_float(dst, tmp, src):
                v.tensor_scalar(tmp, src, 31, 0x7FFFFFFF, ALU.arith_shift_right, ALU.bitwise_and)
                settle()
                v.tensor_tensor(dst, src, tmp, ALU.bitwise_xor)
                settle()

            def round_of(r, steps_r):
                v.tensor_tensor(hit[:, :, :, :], bc(zs[:, :, :].unsqueeze(2), [P, E, CAND, NT]),
                                bc(candf[:, :, :].bitcast(F32).unsqueeze(3), [P, E, CAND, NT]), ALU.is_ge).then_inc(r_hit, 1)
                dve.wait_ge(r_cnt, r + 1)
                v.tensor_scalar(reach[:, :, :].rearrange("p e c -> p (e c)"), counts, float(CAP), -1.0, ALU.is_ge, ALU.mult)
                settle()
                v.tensor_tensor(reach[:, :, :], reach[:, :, :], bc(steps_r, [P, E, CAND]), ALU.bitwise_and)
                settle()
                v.tensor_reduce(dbits[:, :], reach[:, :, :], AX.X, ALU.bitwise_xor)
                settle()
                v.tensor_tensor(thr[:, :], thr[:, :], dbits[:, :], ALU.bitwise_xor)
                settle()

            def candidates(digs_r):
                v.tensor_tensor(candf[:, :, :], bc(thr[:, :].unsqueeze(2), [P, E, CAND]), bc(digs_r, [P, E, CAND]), ALU.bitwise_xor)
                settle()

            candidates(digs[:, 0:1, 1:])
            as_float(candf[:, :, :], fold[:, :, :], candf[:, :, :])
            round_of(0, steps[:, 0:1, :])
            as_float(thr[:, :], dbits[:, :], thr[:, :])
            with dve.Fori(1, ROUNDS) as r:
                candidates(digs[:, bass.ds(r, 1), 1:])
                round_of(r, steps[:, bass.ds(r, 1), :])

            def per_expert(ap):
                return bc(ap.unsqueeze(2), [P, E, NT])

            def flat(ap):
                return ap.rearrange("p e t -> p (e t)")

            def running(flags_total):
                v.tensor_copy(flat(tot[:, :, :]), flags_total)
                settle()
                v.tensor_tensor_scan(flat(cum[:, :, :]), flat(nofirst[:, :, :]), flat(tot[:, :, :]), 0.0, ALU.mult, ALU.add)
                settle()
                v.tensor_tensor(cum[:, :, :], cum[:, :, :], tot[:, :, :], ALU.subtract)
                settle()
                v.tensor_tensor(flat(rank[:, :, :]), flat(cum[:, :, :]), prefix_ps, ALU.add)
                settle()

            v.tensor_tensor(above[:, :, :], zs[:, :, :], per_expert(thr[:, :].bitcast(F32)), ALU.is_gt)
            v.tensor_tensor(tie[:, :, :], zs[:, :, :], per_expert(thr[:, :].bitcast(F32)), ALU.is_equal).then_inc(r_tie, 1)
            dve.wait_ge(r_tieP, 1)
            v.tensor_reduce(room[:, :], above_ps.rearrange("p (e t) -> p e t", t=NT), AX.X, ALU.add)
            settle()
            v.tensor_scalar(room[:, :], room[:, :], -1.0, float(CAP), ALU.mult, ALU.add)
            running(total_ps)
            v.tensor_tensor(key[:, :, :], rank[:, :, :], per_expert(room[:, :]), ALU.is_lt)
            settle()
            v.tensor_tensor(key[:, :, :], key[:, :, :], tie[:, :, :], ALU.mult)
            settle()
            v.tensor_tensor(kept[:, :, :], key[:, :, :], above[:, :, :], ALU.add).then_inc(r_kept, 1)

            v.tensor_copy(wrest[:, :, :], wt[:, :, :])
            settle()
            for i in range(3):
                v.tensor_copy(wpart[:, :, :], wrest[:, :, :])
                settle()
                v.tensor_copy(vals[:, :, :, 2 + i], wpart[:, :, :])
                v.tensor_tensor(wrest[:, :, :], wrest[:, :, :], wpart[:, :, :], ALU.subtract)
                settle()

            dve.wait_ge(r_keptP, 1)
            running(total_ps)
            v.tensor_copy(slot[:, :, :], rank[:, :, :])
            settle()
            v.tensor_scalar(slf[:, :, :], slot[:, :, :], P - 1, None, ALU.bitwise_and)
            v.tensor_scalar(slot[:, :, :], slot[:, :, :], 7, None, ALU.logical_shift_right)
            settle()
            v.tensor_copy(slg[:, :, :], slot[:, :, :])
            v.scalar_tensor_tensor(key[:, :, :], slf[:, :, :], 1.0, kept[:, :, :], ALU.add, ALU.mult)
            settle()
            v.tensor_scalar(slo[:, :, :], key[:, :, :], -1.0, None, ALU.add)
            for g in range(GE):
                v.tensor_scalar(ing[:, :, :], slg[:, :, :], float(g), None, ALU.is_equal)
                settle()
                v.tensor_tensor(place[:, :, :, g * NV:(g + 1) * NV].rearrange("p e t n -> p (e t) n"),
                                vals[:, :, :, :].rearrange("p e t n -> p (e t) n"),
                                bc(flat(ing[:, :, :]).unsqueeze(2), [P, E * NT, NV]), ALU.mult)
                settle()
            dve.wait_ge(st_h, 16 * NB)
            for e in range(E):
                if e >= 2:
                    dve.wait_ge(r_slot, e - 1)
                v.tensor_tensor(hot[:, e % 2, :, :], bc(slo[:, e:e + 1, :], [P, P, NT]), iota_s[:, :, :],
                                ALU.is_equal).then_inc(r_hot, 1)
            dve.wait_ge(r_slot, E)
            v.tensor_copy(slots[:, :, :, :].rearrange("p e g n -> p (e g n)"), slots_ps)
            settle()
            sl = slots[:, :, :, :].rearrange("p e g n -> p (e g) n")
            v.scalar_tensor_tensor(tokf[:, :], sl[:, :, 0], float(P), sl[:, :, 1], ALU.mult, ALU.add)
            v.tensor_reduce(wslot[:, :], sl[:, :, 2:NV], AX.X, ALU.add)
            settle()
            v.tensor_copy(tok[:, :], tokf[:, :]).then_inc(r_idx, 1)

            def gathered_lower(e):
                for k in range(KD):
                    dve.wait_ge(f_hi, KD * e + k + 1)
                    v.tensor_tensor(hgT[1][:, k, :], bank[k][:, 0:CAP], hgT[0][:, k, :].bitcast(F32), ALU.subtract).then_inc(f_hgT, 1)

            def lower_w1(n, w1, k):
                dve.wait_ge(w1_hi, W1N * n + k + 1)
                v.tensor_tensor(w1[1][:, k, :], w1_raw[:, k, :], w1[0][:, k, :].bitcast(F32), ALU.subtract).then_inc(w1_lo, 1)

            def lower_w2(n, w2, k):
                dve.wait_ge(w2_hi, W2N * n + k + 1)
                v.tensor_tensor(w2[1][:, k, :], w2_raw[:, k, :], w2[0][:, k, :].bitcast(F32), ALU.subtract).then_inc(w2_lo, 1)

            def routed_gate(e, half):
                dve.wait_ge(f_th, 2 * e + half + 1)
                v.scalar_tensor_tensor(th[:, half, 0:CAP], th[:, half, 0:CAP], 1.0, bank[4 + 2 * half][:, 0:CAP],
                                       ALU.add, ALU.mult)
                settle()
                dve.wait_ge(q_x1, 2 * e + half + 1)
                v.scalar_tensor_tensor(gf[:, half, 0:CAP], th[:, half, 0:CAP], 0.5, bank[5 + 2 * half][:, 0:CAP],
                                       ALU.mult, ALU.mult).then_inc(f_g, 1)

            def routed_gate_lower(e, half):
                dve.wait_ge(f_ghi, 2 * e + half + 1)
                v.tensor_tensor(gT[1][:, half, 0:CAP], gf[:, half, 0:CAP], gT[0][:, half, 0:CAP].bitcast(F32),
                                ALU.subtract).then_inc(f_glo, 1)

            def expert(e, par):
                last = isinstance(e, int) and e == E - 1
                gathered_lower(e)
                if not last:
                    for k in range(KD - 1):
                        lower_w1(e + 2, w1r[1 - par], k)
                routed_gate(e, 0)
                if not last:
                    lower_w1(e + 2, w1r[1 - par], KD - 1)
                routed_gate_lower(e, 0)
                routed_gate(e, 1)
                if not last:
                    lower_w2(e + 2, w2r[1 - par], 0)
                routed_gate_lower(e, 1)
                if not last:
                    lower_w2(e + 2, w2r[1 - par], 1)

            dve.wait_ge(w2_lo, 2 * W2N)
            expert(0, 0)
            with dve.Fori(1, E - 2, 2) as e:
                expert(e, 1)
                expert(e + 1, 0)
            expert(E - 2, 1)
            expert(E - 1, 0)


_INS = ["x", "ctx_512", "g_xattn", "g_ffn", "L0_xattn_W_k", "L0_xattn_b_k", "L0_xattn_ln_gamma",
        "L0_xattn_ln_beta", "L0_ffn_gate_w", "L0_ffn_expert_bias", "L0_ffn_shared_w1",
        "L0_ffn_shared_w2", "L0_ffn_routed_w1", "L0_ffn_routed_w2"]


def kernel(**inputs):
    import concourse.bacc as bacc
    from concourse.bass_utils import run_bass_kernel_spmd

    nc = bacc.Bacc("TRN2", target_bir_lowering=False, num_devices=1)
    arrays, args = {}, []
    for name in _INS:
        a = np.ascontiguousarray(inputs[name])
        arrays[f"in_{name}"] = a
        args.append(nc.dram_tensor(f"in_{name}", a.shape, mybir.dt.from_np(a.dtype), kind="ExternalInput").ap())
    args.append(nc.dram_tensor("out_0", (NB, S, D), F32, kind="ExternalOutput").ap())
    build(nc, *args)
    r = run_bass_kernel_spmd(nc, [arrays], core_ids=[0])
    return r.results[0]["out_0"]
```

```python
from contextlib import ExitStack

import numpy as np
import concourse.bass as bass
from concourse import mybir

F32 = mybir.dt.float32
F32R = mybir.dt.float32r
BF16 = mybir.dt.bfloat16
I32 = mybir.dt.int32
U32 = mybir.dt.uint32
U8 = mybir.dt.uint8
ALU = mybir.AluOpType
ACT = mybir.ActivationFunctionType
AX = mybir.AxisListType

P = 128
NB = 4
S = 512
D = 512
C = 128
T = NB * S
TT = S // P
NT = T // P
KD = D // P
F = 256
E = 7
CAP = T // E
GE = -(-CAP // P)
GSZ = [min(P, CAP - g * P) for g in range(GE)]
SIM_SCALE2 = 512.0
EPS_SIM = 1e-6
EPS_LN = 1e-5
LEVELS = 4
NIBBLE = 16
CAND = NIBBLE - 1
ROUNDS = 2 * LEVELS
W1N, W2N = KD, 2
NV = 5


def build(nc, x, ctx_in, g_x, g_f, W_k, b_k, gamma, beta, gate_w, ebias, sw1, sw2, rw1, rw2, out):
    with ExitStack() as stack:
        def alloc(where, name, shape, dt=F32):
            return where.enter_context(nc.sbuf_tensor(name, shape, dt))

        def sb(name, shape, dt=F32):
            return alloc(stack, name, shape, dt)

        def pair(where, name, shape):
            return [alloc(where, f"{name}_{part}", shape, F32R) for part in ("hi", "lo")]

        def sem(name):
            return stack.enter_context(nc.semaphore(name))

        bank = [stack.enter_context(nc.psum_tensor(f"bank{i}", [P, 512], F32)) for i in range(8)]
        h_dram = nc.dram_tensor("h_rows", [T, D], F32, kind="Internal").ap()

        ident = sb("ident", [P, P])
        later = sb("later", [P, P], BF16)
        ones = sb("ones", [P, P], BF16)
        minus = sb("minus", [P, P], BF16)
        WkT = sb("WkT", [P, C])
        bk_col = sb("bk_col", [P, 1])
        gates = sb("gates", [P, 2])
        gt = sb("gt", [P, 2])
        eb = sb("eb", [P, E])
        w1_raw = sb("w1_raw", [P, KD, 2 * F])
        w2_raw = sb("w2_raw", [P, 2, D])
        w1s = pair(stack, "w1s", [P, KD, 2 * F])
        w2s = pair(stack, "w2s", [P, 2, D])
        w1r = [pair(stack, "w1r0", [P, KD, 2 * F])]
        w2r = [pair(stack, "w2r0", [P, 2, D])]
        xs = sb("xs", [P, NT, D])
        hT = pair(stack, "hT", [P, KD, S])
        th = sb("th", [P, 2, S])
        gf = sb("gf", [P, 2, S])
        gT = pair(stack, "gT", [P, 2, S])
        z = sb("z", [P, E, NT])
        z2 = sb("z2", [P, E, NT])
        m1 = sb("m1", [P, NT])
        eq = sb("eq", [P, E, NT])
        key = sb("key", [P, E, NT])
        one = sb("one", [P, 2, E, NT])
        mask = sb("mask", [P, E, NT])
        pref = sb("pref", [P, E, 1])
        prefi = sb("prefi", [P, E, 1], I32)
        signs = sb("signs", [P, E, NT], I32)
        ordered = sb("ordered", [P, E, NT], I32)
        plane = sb("plane", [P, LEVELS, E, NT], BF16)
        wt = sb("wt", [P, E, NT])
        wpart = sb("wpart", [P, E, NT], BF16)
        high = sb("high", [P, CAND, NT], BF16)
        low = sb("low", [P, CAND, NT], BF16)
        rest = sb("rest", [P, E, NT], BF16)
        above_by = sb("above_by", [P, E, NT], BF16)
        reach = sb("reach", [P, E, CAND])
        digit = sb("digit", [P, E])
        flags = sb("flags", [P, 2, E, NT], BF16)
        cum = sb("cum", [P, 2, E, NT])
        rank = sb("rank", [P, 2, E, NT])
        room = sb("room", [P, E])
        nofirst = sb("nofirst", [P, 2, E, NT])
        fits = sb("fits", [P, E, NT])
        before = sb("before", [P, E, NT])
        kept = sb("kept", [P, E, NT])
        slot = sb("slot", [P, E, NT], I32)
        slf = sb("slf", [P, E, NT], I32)
        slg = sb("slg", [P, E, NT], I32)
        slgf = sb("slgf", [P, E, NT], BF16)
        group = sb("group", [P, GE, E * NT], BF16)
        row1 = sb("row1", [P, E, NT])
        rowc = sb("rowc", [P, 2, E, NT])
        srow = sb("srow", [P, 2, NT], BF16)
        iota_s = sb("iota_s", [P, P, NT], BF16)
        row_i = sb("row_i", [P, 1], I32)
        row_f = sb("row_f", [P, 1])
        tile_i = sb("tile_i", [P, NT], I32)
        tile_f = sb("tile_f", [P, NT])
        told = sb("told", [P, 2 * NV, E * NT], BF16)
        ing = sb("ing", [P, GE, E * NT], BF16)
        slots = sb("slots", [P, NV, GE * E])
        tok = sb("tok", [P, GE * E], I32)
        wsum = sb("wsum", [P, GE * E])
        wslot = sb("wslot", [P, GE * E])
        kvsum = sb("kvsum", [P, 1])
        ssq = sb("ssq", [P, TT])
        bnx = sb("bnx", [P, TT, 6])
        mvx = sb("mvx", [P, TT, 2])
        vq = sb("vq", [P, TT])
        vs = sb("vs", [P, TT])
        rs = sb("rs", [P, TT])
        mhalf = sb("mhalf", [P, TT])
        nmax = sb("nmax", [P, TT])
        esum = sb("esum", [P, TT])
        coef = sb("coef", [P, TT])
        bnh = sb("bnh", [P, TT, 6])
        mvh = sb("mvh", [P, TT, 2])
        vh = sb("vh", [P, TT])
        rh = sb("rh", [P, TT])

        with ExitStack() as early:
            xb = alloc(early, "xb", [P, TT, D])
            prob = alloc(early, "prob", [P, TT, S])
            ctxb = alloc(early, "ctxb", [P, TT, C])
            gamma_b = alloc(early, "gamma_b", [P, S])
            beta_b = alloc(early, "beta_b", [P, S])
            h = alloc(early, "h", [P, TT, D])
            ctxT = alloc(early, "ctxT", [P, S])
            kvT = alloc(early, "kvT", [P, S])
            kvcT = alloc(early, "kvcT", [P, S])
            kvc = alloc(early, "kvc", [P, TT, C])
            xT = alloc(early, "xT", [P, TT, S])
            outT = alloc(early, "outT", [P, S])
            Wk_rows = alloc(early, "Wk_rows", [P, C])
            gw_raw = alloc(early, "gw_raw", [P, KD, P])
            gw = pair(early, "gw", [P, KD, P])
            zT = alloc(early, "zT", [P, S])
        with ExitStack() as late:
            w1r.append(pair(late, "w1r1", [P, KD, 2 * F]))
            w2r.append(pair(late, "w2r1", [P, 2, D]))
            xg = [alloc(late, f"xg{i}", [P, GE, D]) for i in range(2)]
            yr = [alloc(late, f"yr{i}", [P, GE, D]) for i in range(2)]
            hgT = pair(late, "hgT", [P, KD, CAP])
        with ExitStack() as between:
            hot = alloc(between, "hot", [P, 2, P, NT], BF16)
            place = alloc(between, "place", [P, 2 * NV, GE, E * NT], BF16)
            hit = alloc(between, "hit", [P, E, CAND, NT], BF16)

        block = stack.enter_context(nc.Block())

        ld_wk, ld_rows, ld_ctx, ld_xb, ld_w1, ld_w2 = (sem(n) for n in
            ("ld_wk", "ld_rows", "ld_ctx", "ld_xb", "ld_w1", "ld_w2"))
        ld_x = [sem(f"ld_x{i}") for i in range(NB)]
        st_h = sem("st_h")
        st_out = sem("st_out")
        gath = [sem(f"gath{i}") for i in range(2)]
        scat = [sem(f"scat{i}") for i in range(2)]
        y_landed = sem("y_landed")
        c_pool, c_iota, c_wk, c_wkT, c_tanh, c_gw = (sem(n) for n in ("c_pool", "c_iota", "c_wk", "c_wkT", "c_tanh", "c_gw"))
        w1_hi, w1_lo, w2_hi, w2_lo = (sem(n) for n in ("w1_hi", "w1_lo", "w2_hi", "w2_lo"))
        p_ctxT, p_xT, p_kvT, p_kvc, p_outT, p_S = (sem(n) for n in
            ("p_ctxT", "p_xT", "p_kvT", "p_kvc", "p_outT", "p_S"))
        e_ctxT, e_xT, e_kvT, e_kvcT, e_kvc, e_outT = (sem(n) for n in
            ("e_ctxT", "e_xT", "e_kvT", "e_kvcT", "e_kvc", "e_outT"))
        e_ssq, e_vs, e_rs, e_scaled, e_logit, e_exp, e_vh, e_rh, e_h = (sem(n) for n in
            ("e_ssq", "e_vs", "e_rs", "e_scaled", "e_logit", "e_exp", "e_vh", "e_rh", "e_h"))
        p_hT, p_zT, p_z, p_x2, p_x1, p_y = (sem(n) for n in ("p_hT", "p_zT", "p_z", "p_x2", "p_x1", "p_y"))
        e_hi, e_hT, e_zT, e_z, e_th, e_u, e_g, e_ghi, e_glo, e_y = (sem(n) for n in
            ("e_hi", "e_hT", "e_zT", "e_z", "e_th", "e_u", "e_g", "e_ghi", "e_glo", "e_y"))
        r_sig, r_one, r_told, r_hit, r_cnt, r_flags, r_flagsP, r_hot, r_slot, r_idx = (sem(n) for n in
            ("r_sig", "r_one", "r_told", "r_hit", "r_cnt", "r_flags", "r_flagsP", "r_hot", "r_slot", "r_idx"))
        q_hgT, q_x2, q_x1, q_y = (sem(n) for n in ("q_hgT", "q_x2", "q_x1", "q_y"))
        f_hi, f_hgT, f_th, f_g, f_ghi, f_glo, f_y = (sem(n) for n in
            ("f_hi", "f_hgT", "f_th", "f_g", "f_ghi", "f_glo", "f_y"))

        def bc(ap, shape):
            return ap.broadcast_to(shape)

        counts = bank[7][:, 0:E * CAND]
        zps = bank[7][:, :].rearrange("p (t e) -> p t e", e=P)
        total_ps = bank[7][:, 0:2 * E * NT]
        prefix_ps = bank[7][:, 2 * E * NT:4 * E * NT]
        slots_ps = bank[0][:, 0:NV * GE * E]

        HT_BANK = (4, 6, 5, 4)
        X2_BANK, X1_BANK = (5, 6), (4, 5)
        Y_BANK = (6, 4, 5, 6)

        @block.sync
        def _(sp):
            def row(v, n):
                return v.rearrange("(o n) -> o n", o=1).broadcast_to([P, n])

            sp.dma_start(ctxb[:, :, :], ctx_in[0].rearrange("(t p) c -> p t c", p=P)).then_inc(ld_ctx, 16)
            sp.dma_start(Wk_rows[:, :], W_k).then_inc(ld_wk, 16)
            sp.dma_start(xb[:, :, :], x[0].rearrange("(t p) d -> p t d", p=P)).then_inc(ld_xb, 16)
            sp.dma_start(bk_col[:, :], b_k.rearrange("(p o) -> p o", o=1)).then_inc(ld_wk, 16)
            sp.dma_start(xs[:, 0:TT, :], x[0].rearrange("(t p) d -> p t d", p=P)).then_inc(ld_x[0], 16)
            sp.dma_start(gamma_b[:, :], row(gamma, S)).then_inc(ld_rows, 16)
            sp.dma_start(beta_b[:, :], row(beta, S)).then_inc(ld_rows, 16)
            sp.dma_start(gates[:, 0:1], row(g_x, 1)).then_inc(ld_rows, 16)
            sp.dma_start(gates[:, 1:2], row(g_f, 1)).then_inc(ld_rows, 16)
            sp.dma_start(eb[:, :], row(ebias, E)).then_inc(ld_rows, 16)
            sp.wait_ge(c_gw, 1)
            sp.dma_start(gw_raw[:, :, 0:E], gate_w.rearrange("(k p) e -> p k e", p=P)).then_inc(ld_rows, 16)
            sp.dma_start(w1_raw[:, :, :], sw1[0].rearrange("(k p) f -> p k f", p=P)).then_inc(ld_w1, 16)
            sp.dma_start(w2_raw[:, :, :], sw2[0].rearrange("(k p) d -> p k d", p=P)).then_inc(ld_w2, 16)
            for b in range(1, NB):
                sp.dma_start(xs[:, b * TT:(b + 1) * TT, :], x[b].rearrange("(t p) d -> p t d", p=P)).then_inc(ld_x[b], 16)
            h_rows = h_dram.rearrange("(b t p) d -> b p t d", p=P, t=TT)
            out_rows = out.rearrange("b (t p) d -> b p t d", p=P)
            ctx_rows = ctx_in.rearrange("b (t p) c -> b p t c", p=P)
            x_rows = x.rearrange("b (t p) d -> b p t d", p=P)
            with sp.Fori(0, NB - 1) as b:
                sp.wait_ge(p_ctxT, b + 1)
                sp.dma_start(ctxb[:, :, :], ctx_rows[bass.ds(b + 1, 1), :, :, :].rearrange("o p t c -> (o p) t c")).then_inc(ld_ctx, 16)
                sp.wait_ge(p_xT, TT * b + TT)
                sp.dma_start(xb[:, :, :], x_rows[bass.ds(b + 1, 1), :, :, :].rearrange("o p t d -> (o p) t d")).then_inc(ld_xb, 16)
                sp.wait_ge(e_h, b + 1)
                sp.dma_start(h_rows[bass.ds(b, 1), :, :, :].rearrange("o p t d -> (o p) t d"), h[:, :, :]).then_inc(st_h, 16)
            sp.wait_ge(w1_lo, W1N)
            sp.wait_ge(w2_lo, W2N)
            sp.dma_start(w1_raw[:, :, :], rw1[0].rearrange("(k p) f -> p k f", p=P)).then_inc(ld_w1, 16)
            sp.dma_start(w2_raw[:, :, :], rw2[0].rearrange("(k p) d -> p k d", p=P)).then_inc(ld_w2, 16)
            sp.wait_ge(e_h, NB)
            sp.dma_start(h_rows[NB - 1], h[:, :, :]).then_inc(st_h, 16)
            with sp.Fori(0, NB) as b:
                sp.wait_ge(e_y, TT * b + 2 * TT)
                sp.dma_start(out_rows[bass.ds(b, 1), :, :, :].rearrange("o p t d -> (o p) t d"),
                             xs[:, bass.ds(b * TT, TT), :]).then_inc(st_out, 16)
            w1_rows = rw1.rearrange("e (k p) f -> e p k f", p=P)
            w2_rows = rw2.rearrange("e (k p) d -> e p k d", p=P)
            with sp.Fori(1, E) as e:
                sp.wait_ge(w1_lo, W1N * e + W1N)
                sp.dma_start(w1_raw[:, :, :], w1_rows[bass.ds(e, 1), :, :, :].rearrange("o p k f -> (o p) k f")).then_inc(ld_w1, 16)
                sp.wait_ge(w2_lo, W2N * e + W2N)
                sp.dma_start(w2_raw[:, :, :], w2_rows[bass.ds(e, 1), :, :, :].rearrange("o p k d -> (o p) k d")).then_inc(ld_w2, 16)

        @block.tensor
        def _(pe):
            def transpose(out_ap, in_ap, n=P):
                return nc.tensor.transpose(out_ap, in_ap, ident[0:n, 0:n])

            def product(out_ap, pieces):
                todo = [(w[i], m[j]) for w, m in pieces for i, j in ((0, 0), (0, 1), (1, 0))]
                for n, (w, m) in enumerate(todo):
                    last = nc.tensor.matmul(out_ap, w, m, start=n == 0, stop=n == len(todo) - 1)
                return last

            def both(p, *at):
                return p[0][at], p[1][at]

            A = slice(None)

            def context(b):
                pe.wait_ge(ld_ctx, 16 * b + 16)
                if not isinstance(b, int) or b > 0:
                    pe.wait_ge(e_scaled, TT * b - 3)
                for t in range(TT):
                    last = transpose(bank[0][:, t * P:(t + 1) * P], ctxb[:, t, :])
                last.then_inc(p_ctxT, 1)

            def x_cols(b, j, bk):
                for t in range(TT):
                    last = transpose(bank[bk][:, t * P:(t + 1) * P], xb[:, t, j * P:(j + 1) * P])
                last.then_inc(p_xT, 1)

            def keys(b):
                later = not isinstance(b, int) or b > 0
                pe.wait_ge(ld_xb, 16 * b + 16)
                if later:
                    pe.wait_ge(e_scaled, TT * b - 2)
                x_cols(b, 0, 1)
                pe.wait_ge(e_ctxT, b + 1)
                if later:
                    pe.wait_ge(e_scaled, TT * b - 1)
                nc.tensor.matmul(bank[2][:, :], WkT[:, :], ctxT[:, :], start=True, stop=True).then_inc(p_kvT, 1)

            def more_x(b):
                if not isinstance(b, int) or b > 0:
                    pe.wait_ge(e_scaled, TT * b)
                x_cols(b, 1, 3)
                x_cols(b, 2, 0)

            def keys_back(b):
                pe.wait_ge(e_kvcT, b + 1)
                pe.wait_ge(e_xT, TT * b + 1)
                for t in range(TT):
                    last = transpose(bank[1][:, t * C:(t + 1) * C], kvcT[:, t * P:(t + 1) * P])
                last.then_inc(p_kvc, 1)
                x_cols(b, 3, 2)

            def attend(b):
                pe.wait_ge(e_kvc, b + 1)
                for j in range(TT):
                    if j != 1:
                        pe.wait_ge(e_xT, TT * b + max(j, 1) + 1)
                    last = nc.tensor.matmul(bank[3][:, :], kvc[:, j, :], xT[:, j, :], start=j == 0, stop=j == TT - 1)
                last.then_inc(p_outT, 1)

            def scores(b):
                pe.wait_ge(e_outT, b + 1)
                for t in range(TT):
                    nc.tensor.matmul(bank[t][:, :], outT[:, t * P:(t + 1) * P], kvcT[:, :], start=True, stop=True).then_inc(p_S, 1)

            def rows_back(f):
                later = not isinstance(f, int) or f > 0
                pe.wait_ge(e_h, f + 1)
                for k in range(KD):
                    if later and k == 0:
                        pe.wait_ge(e_g, 2 * f - 1)
                    if later and k == 1:
                        pe.wait_ge(e_u, 2 * f)
                    if later and k == 2:
                        pe.wait_ge(e_g, 2 * f)
                    if k == 3:
                        pe.wait_ge(e_hT, KD * f + 1)
                    for t in range(TT):
                        last = transpose(bank[HT_BANK[k]][:, t * P:(t + 1) * P], h[:, t, k * P:(k + 1) * P])
                    last.then_inc(p_hT, 1)
                pe.wait_ge(e_hT, KD * f + KD)
                pe.wait_ge(e_z, f + 1)
                product(bank[7][:, :], [(both(gw, A, k, A), both(hT, A, k, A)) for k in range(KD)]).then_inc(p_zT, 1)

            def logits(f):
                pe.wait_ge(e_zT, f + 1)
                for t in range(TT):
                    last = transpose(zps[:, t, :], zT[:, t * P:(t + 1) * P])
                last.then_inc(p_z, 1)

            def up(f):
                for half in range(2):
                    pe.wait_ge(e_y, TT * f + 3 + half)
                    for w_col, bk, done in ((F, X2_BANK[half], p_x2), (0, X1_BANK[half], p_x1)):
                        if half == 1 and done is p_x1:
                            pe.wait_ge(e_u, 2 * f + 1)
                        col = slice(w_col + half * P, w_col + half * P + P)
                        product(bank[bk][:, :], [(both(w1s, A, k, col), both(hT, A, k, A)) for k in range(KD)]).then_inc(done, 1)

            def down(f, t):
                pe.wait_ge(e_glo, 2 * f + 2)
                if t == 3:
                    pe.wait_ge(e_y, TT * f + TT + 1)
                col = slice(t * P, (t + 1) * P)
                product(bank[Y_BANK[t]][:, :], [(both(gT, A, k, col), both(w2s, A, k, A)) for k in range(2)]).then_inc(p_y, 1)

            pe.wait_ge(c_pool, 4)
            pe.wait_ge(ld_wk, 32)
            transpose(bank[7][:, 0:C], Wk_rows[:, :]).then_inc(c_wk, 1)
            context(0)
            pe.wait_ge(c_wkT, 1)
            for b in range(2):
                if b == 1:
                    context(1)
                keys(b)
                more_x(b)
                keys_back(b)
                attend(b)
                if b == 0:
                    scores(0)
            pe.wait_ge(c_gw, 3)
            pe.wait_ge(w1_lo, W1N)
            pe.wait_ge(w2_lo, W2N)
            scores(1)
            rows_back(0)
            logits(0)
            with pe.Fori(2, NB) as b:
                up(b - 2)
                rows_back(b - 1)
                context(b)
                keys(b)
                down(b - 2, 0)
                logits(b - 1)
                more_x(b)
                down(b - 2, 1)
                keys_back(b)
                down(b - 2, 2)
                attend(b)
                down(b - 2, 3)
                scores(b)
            up(NB - 2)
            rows_back(NB - 1)
            down(NB - 2, 0)
            logits(NB - 1)
            for t in range(1, TT):
                down(NB - 2, t)
            up(NB - 1)

            def count(r):
                for half in range(2):
                    pe.wait_ge(r_hit, 2 * r + half + 1)
                    for t in range(half * NT // 2, (half + 1) * NT // 2):
                        last = nc.tensor.matmul(counts, ones[:, :], hit[:, :, :, t], start=t == 0, stop=t == NT - 1)
                last.then_inc(r_cnt, 1)

            for r in range(ROUNDS):
                count(r)
                if r < TT:
                    down(NB - 1, r)
            pe.wait_ge(r_flags, 1)
            both_flags = flags[:, :, :, :].rearrange("p a e t -> p (a e t)")
            nc.tensor.matmul(total_ps, ones[:, :], both_flags, start=True, stop=True)
            nc.tensor.matmul(prefix_ps, later[:, :], both_flags, start=True, stop=True).then_inc(r_flagsP, 1)
            for c in range(2):
                pe.wait_ge(r_hot, c + 1)
                for t in range(NT):
                    last = nc.tensor.matmul(slots_ps, hot[:, c, :, t],
                                            place[:, c * NV:(c + 1) * NV, :, :].rearrange("p n g (e t) -> p (n g e) t", t=NT)[:, :, t],
                                            start=c == 0 and t == 0, stop=c == 1 and t == NT - 1)
            last.then_inc(r_slot, 1)

            def gathered(e, par):
                pe.wait_ge(gath[par], (e - par) * (8 * GE) + 16 * GE)
                for k in range(KD):
                    if not isinstance(e, int) or e > 0:
                        pe.wait_ge(f_hgT, KD * e - KD + k + 1)
                    for g in range(GE):
                        last = transpose(bank[k][:, g * P:g * P + GSZ[g]], xg[par][0:GSZ[g], g, k * P:(k + 1) * P], GSZ[g])
                    last.then_inc(q_hgT, 1)

            def routed_up(e, par):
                pe.wait_ge(f_hgT, KD * e + KD)
                pe.wait_ge(w1_lo, W1N * e + 2 * W1N)
                for half in range(2):
                    for part, (w_col, done) in enumerate(((F, q_x2), (0, q_x1))):
                        bk = 2 * half + part
                        if not isinstance(e, int) or e > 0:
                            pe.wait_ge(f_y, GE * e - GE + bk + 1) if bk < GE else pe.wait_ge(f_g, 2 * e)
                        col = slice(w_col + half * P, w_col + half * P + P)
                        product(bank[4 + bk][:, 0:CAP], [(both(w1r[par], A, k, col), both(hgT, A, k, A)) for k in range(KD)]).then_inc(done, 1)

            def routed_down(e, par):
                pe.wait_ge(f_glo, 2 * e + 2)
                pe.wait_ge(w2_lo, W2N * e + 2 * W2N)
                for g in range(GE):
                    col = slice(g * P, g * P + GSZ[g])
                    product(bank[4 + g][0:GSZ[g], :], [(both(gT, A, k, col), both(w2r[par], A, k, A)) for k in range(2)]).then_inc(q_y, 1)

            pe.wait_ge(e_y, TT * NB + TT)
            gathered(0, 0)
            routed_up(0, 0)
            with pe.Fori(1, E, 2) as e:
                gathered(e, 1)
                routed_down(e - 1, 0)
                routed_up(e, 1)
                gathered(e + 1, 0)
                routed_down(e, 1)
                routed_up(e + 1, 0)
            routed_down(E - 1, 0)

        @block.scalar
        def _(act):
            def copy(dst, src):
                return nc.scalar.activation(dst, src, ACT.Copy)

            def upper_w1(n, w1, k):
                if k == 0:
                    act.wait_ge(ld_w1, 16 * n + 16)
                copy(w1[0][:, k, :], w1_raw[:, k, :]).then_inc(w1_hi, 1)

            def upper_w2(n, w2, k):
                if k == 0:
                    act.wait_ge(ld_w2, 16 * n + 16)
                copy(w2[0][:, k, :], w2_raw[:, k, :]).then_inc(w2_hi, 1)

            def upper_weights(n, w1, w2):
                for k in range(W1N):
                    upper_w1(n, w1, k)
                for k in range(W2N):
                    upper_w2(n, w2, k)

            def x_copy(b, j, bk):
                act.wait_ge(p_xT, TT * b + j + 1)
                copy(xT[:, j, :], bank[bk][:, :]).then_inc(e_xT, 1)

            def front(b):
                act.wait_ge(p_ctxT, b + 1)
                copy(ctxT[:, :], bank[0][:, :]).then_inc(e_ctxT, 1)
                x_copy(b, 0, 1)
                act.wait_ge(p_kvT, b + 1)
                nc.scalar.activation(kvT[:, :], bank[2][:, :], ACT.Identity, bias=bk_col[:, 0:1],
                                     accum_out=kvsum[:, :]).then_inc(e_kvT, 1)
                x_copy(b, 1, 3)
                x_copy(b, 2, 0)
                act.wait_ge(p_kvc, b + 1)
                copy(kvc[:, :, :].rearrange("p t c -> p (t c)"), bank[1][:, :]).then_inc(e_kvc, 1)
                x_copy(b, 3, 2)
                act.wait_ge(p_outT, b + 1)
                copy(outT[:, :], bank[3][:, :]).then_inc(e_outT, 1)

            def squares(b):
                if not isinstance(b, int) or b > 0:
                    act.wait_ge(e_h, b)
                for t in range(TT):
                    act.wait_ge(p_S, TT * b + t + 1)
                    nc.scalar.activation(prob[:, t, :], bank[t][:, :], ACT.Square, accum_out=ssq[:, t:t + 1]).then_inc(e_ssq, 1)

            def exps(b):
                for t in range(TT):
                    act.wait_ge(e_logit, TT * b + t + 1)
                    nc.scalar.activation(prob[:, t, :], prob[:, t, :], ACT.Exp, bias=nmax[:, t:t + 1], scale=-1.0,
                                         accum_out=esum[:, t:t + 1]).then_inc(e_exp, 1)

            def rows_upper(f):
                for k in range(KD):
                    act.wait_ge(p_hT, KD * f + k + 1)
                    copy(hT[0][:, k, :], bank[HT_BANK[k]][:, :]).then_inc(e_hi, 1)
                act.wait_ge(p_zT, f + 1)
                copy(zT[:, :], bank[7][:, :]).then_inc(e_zT, 1)

            def gate_tanh(f, half):
                act.wait_ge(p_x2, 2 * f + half + 1)
                nc.scalar.activation(th[:, half, :], bank[X2_BANK[half]][:, :], ACT.Tanh, scale=0.5).then_inc(e_th, 1)

            def gate_upper(f, half):
                act.wait_ge(e_g, 2 * f + half + 1)
                copy(gT[0][:, half, :], gf[:, half, :]).then_inc(e_ghi, 1)

            act.wait_ge(c_wk, 1)
            copy(WkT[:, :], bank[7][:, 0:C]).then_inc(c_wkT, 1)
            front(0)
            act.wait_ge(ld_rows, 16 * 6)
            nc.scalar.activation(gt[:, :], gates[:, :], ACT.Tanh).then_inc(c_tanh, 1)
            squares(0)
            copy(gw[0][:, :, :], gw_raw[:, :, :]).then_inc(c_gw, 1)
            upper_weights(0, w1s, w2s)
            exps(0)
            front(1)
            squares(1)
            rows_upper(0)
            with act.Fori(2, NB) as b:
                gate_tanh(b - 2, 0)
                exps(b - 1)
                gate_upper(b - 2, 0)
                gate_tanh(b - 2, 1)
                gate_upper(b - 2, 1)
                rows_upper(b - 1)
                front(b)
                squares(b)
            gate_tanh(NB - 2, 0)
            exps(NB - 1)
            gate_upper(NB - 2, 0)
            gate_tanh(NB - 2, 1)
            gate_upper(NB - 2, 1)
            rows_upper(NB - 1)
            gate_tanh(NB - 1, 0)
            act.wait_ge(e_z, NB + 1)
            nc.scalar.activation(wt[:, :, :].rearrange("p e t -> p (e t)"), z[:, :, :].rearrange("p e t -> p (e t)"),
                                 ACT.Tanh, scale=0.5).then_inc(r_sig, 1)
            gate_upper(NB - 1, 0)
            gate_tanh(NB - 1, 1)
            gate_upper(NB - 1, 1)
            upper_weights(1, w1r[0], w2r[0])

            def gathered_upper(e):
                for k in range(KD):
                    act.wait_ge(q_hgT, KD * e + k + 1)
                    copy(hgT[0][:, k, :], bank[k][:, 0:CAP]).then_inc(f_hi, 1)

            def routed_tanh(e, half):
                act.wait_ge(q_x2, 2 * e + half + 1)
                nc.scalar.activation(th[:, half, 0:CAP], bank[4 + 2 * half][:, 0:CAP], ACT.Tanh, scale=0.5).then_inc(f_th, 1)

            def routed_gate_upper(e, half):
                act.wait_ge(f_g, 2 * e + half + 1)
                copy(gT[0][:, half, 0:CAP], gf[:, half, 0:CAP]).then_inc(f_ghi, 1)

            def scaled(e, par, g):
                if g == 0:
                    act.wait_ge(y_landed, e + 1)
                act.wait_ge(q_y, GE * e + g + 1)
                w = wslot[0:GSZ[g], g * E + e:g * E + e + 1] if isinstance(e, int) else wslot[0:GSZ[g], bass.ds(e + g * E, 1)]
                nc.scalar.activation(yr[par][0:GSZ[g], g, :], bank[4 + g][0:GSZ[g], :], ACT.Copy, scale=w).then_inc(f_y, 1)

            def expert(e, par):
                first, last = isinstance(e, int) and e == 0, isinstance(e, int) and e == E - 1
                w1, w2 = w1r[1 - par], w2r[1 - par]
                gathered_upper(e)
                for g in range(GE):
                    if not last:
                        upper_w1(e + 2, w1, g)
                    if not first:
                        scaled(e - 1, 1 - par, g)
                routed_tanh(e, 0)
                if not last:
                    upper_w1(e + 2, w1, KD - 1)
                routed_gate_upper(e, 0)
                routed_tanh(e, 1)
                if not last:
                    upper_w2(e + 2, w2, 0)
                    upper_w2(e + 2, w2, 1)
                routed_gate_upper(e, 1)

            act.wait_ge(r_idx, 1)
            expert(0, 0)

            with act.Fori(1, E - 2, 2) as e:
                expert(e, 1)
                expert(e + 1, 0)
            expert(E - 2, 1)
            expert(E - 1, 0)
            for g in range(GE):
                scaled(E - 1, 0, g)

        @block.gpsimd
        def _(pool):
            g_ = nc.gpsimd
            g_.memset(ident[:, :], 0.0)
            g_.memset(ones[:, :], 1.0).then_inc(c_pool, 1)
            g_.memset(minus[:, :], -1.0)
            g_.memset(mhalf[:, :], -0.5).then_inc(c_pool, 1)
            g_.memset(gw_raw[:, :, :], 0.0).then_inc(c_gw, 1)
            g_.drain()
            g_.affine_select(out=ident[:, :], in_=ident[:, :], compare_op=ALU.not_equal, fill=1.0, base=0,
                             pattern=[[-1, P]], channel_multiplier=1).then_inc(c_pool, 1)
            g_.affine_select(out=later[:, :], in_=minus[:, :], compare_op=ALU.is_ge, fill=0.0, base=0,
                             pattern=[[-1, P]], channel_multiplier=1).then_inc(c_pool, 1)
            g_.iota(prefi[:, :, 0], [[-1, E]], base=E, channel_multiplier=0).then_inc(c_iota, 1)
            g_.iota(row_i[:, :], [[0, 1]], base=0, channel_multiplier=1).then_inc(c_iota, 1)
            g_.iota(tile_i[:, :], [[1, NT]], base=0, channel_multiplier=0).then_inc(c_iota, 1)
            for step, dst in ((NIBBLE, high), (1, low)):
                g_.iota(dst[:, :, :], [[step, CAND], [0, NT]], base=step, channel_multiplier=0,
                        allow_small_or_imprecise_dtypes=True).then_inc(c_iota, 1)
            g_.iota(group[:, :, :], [[1, GE], [0, E * NT]], base=0, channel_multiplier=0,
                    allow_small_or_imprecise_dtypes=True).then_inc(c_iota, 1)
            g_.iota(iota_s[:, :, :], [[1, P], [0, NT]], base=1, channel_multiplier=0,
                    allow_small_or_imprecise_dtypes=True).then_inc(c_iota, 1)

            def inverse_root_scores(b):
                pool.wait_ge(e_vs, b + 1)
                g_.tensor_tensor(rs[:, :], vs[:, :], mhalf[:, :], ALU.pow).then_inc(e_rs, 1)

            def inverse_root_rows(b):
                pool.wait_ge(e_vh, b + 1)
                g_.tensor_tensor(rh[:, :], vh[:, :], mhalf[:, :], ALU.pow).then_inc(e_rh, 1)

            def lower_weights(n, w1, w2):
                for w, raw, pieces, hi, lo in ((w1, w1_raw, W1N, w1_hi, w1_lo), (w2, w2_raw, W2N, w2_hi, w2_lo)):
                    for k in range(pieces):
                        pool.wait_ge(hi, pieces * n + k + 1)
                        g_.tensor_tensor(w[1][:, k, :], raw[:, k, :], w[0][:, k, :].bitcast(F32), ALU.subtract).then_inc(lo, 1)

            inverse_root_scores(0)
            lower_weights(0, w1s, w2s)
            inverse_root_rows(0)
            with pool.Fori(1, NB) as b:
                inverse_root_scores(b)
                inverse_root_rows(b)

            pool.wait_ge(r_one, 1)
            def tell(n, ap):
                told_n = told[:, :, :].rearrange("p (c n) (e t) -> p n c e t", n=NV, t=NT)[:, n, :, :, :]
                return g_.tensor_tensor(told_n, one[:, :, :, :], ap, ALU.mult)

            tell(0, bc(tile_f[:, :].unsqueeze(1).unsqueeze(1), [P, 2, E, NT]))
            tell(1, bc(row_f[:, :].unsqueeze(1).unsqueeze(1), [P, 2, E, NT]))
            pool.wait_ge(r_sig, 1)
            g_.tensor_scalar(wt[:, :, :], wt[:, :, :], 0.5, 0.5, ALU.mult, ALU.add)
            g_.drain()
            g_.tensor_scalar(wt[:, :, :], wt[:, :, :], gt[:, 1:2], None, ALU.mult)
            g_.drain()
            for i in range(3):
                g_.tensor_copy(wpart[:, :, :], wt[:, :, :])
                g_.drain()
                last = tell(2 + i, bc(wpart[:, :, :].unsqueeze(1), [P, 2, E, NT]))
                g_.tensor_tensor(wt[:, :, :], wt[:, :, :], wpart[:, :, :], ALU.subtract)
                g_.drain()
            last.then_inc(r_told, 1)
            lower_weights(1, w1r[0], w2r[0])

            pool.wait_ge(st_h, 16 * NB)
            pool.wait_ge(r_idx, 1)

            def index(e, g):
                return bass.IndirectOffsetOnAxis(ap=tok[0:GSZ[g], g * E + e:g * E + e + 1].bitcast(U32), axis=0)

            def gather(e):
                for g in range(GE):
                    g_.indirect_dma_start(xg[e % 2][0:GSZ[g], g, :], None, h_dram, index(e, g),
                                          bounds_check=T - 1).then_inc(gath[e % 2], 16)

            rows = out.rearrange("b s d -> (b s) d")
            g_.sem_inc(y_landed, 2)
            gather(0)
            gather(1)
            pool.wait_ge(st_out, 16 * NB)
            for e in range(E):
                if e + 2 < E:
                    pool.wait_ge(q_hgT, KD * e + KD)
                    gather(e + 2)
                if e >= 1:
                    pool.wait_ge(scat[(e - 1) % 2], 16 * GE * ((e - 1) // 2 + 1))
                    g_.sem_inc(y_landed, 1)
                pool.wait_ge(f_y, GE * (e + 1))
                for g in range(GE):
                    g_.indirect_dma_start(rows, index(e, g), yr[e % 2][0:GSZ[g], g, :], None, bounds_check=T - 1,
                                          compute_op=ALU.add).then_inc(scat[e % 2], 16)
            for i in range(2):
                pool.wait_ge(scat[i], 16 * GE * len(range(i, E, 2)))

        @block.vector
        def _(dve):
            v = nc.vector

            def settle():
                return v.drain()

            v.sem_inc(e_y, TT)
            v.sem_inc(e_z, 1)

            def tile_of(t):
                return xs[:, t, :] if isinstance(t, int) else xs[:, bass.ds(t, 1), :].rearrange("p o d -> p (o d)")

            def x_stats(b):
                for t in range(TT):
                    v.bn_stats(bnx[:, t, :], tile_of(b * TT + t))
                settle()
                for t in range(TT):
                    v.bn_aggr(mvx[:, t, :], bnx[:, t, :])
                settle()
                v.tensor_scalar(vq[:, :], mvx[:, :, 1], EPS_LN, EPS_SIM * SIM_SCALE2, ALU.add, ALU.mult)

            def centre_keys(b):
                dve.wait_ge(e_kvT, b + 1)
                v.tensor_scalar(kvsum[:, :], kvsum[:, :], 1.0 / S, None, ALU.mult)
                settle()
                v.tensor_scalar(kvcT[:, :], kvT[:, :], kvsum[:, 0:1], None, ALU.subtract).then_inc(e_kvcT, 1)

            def score_variance(b):
                dve.wait_ge(e_ssq, TT * b + TT)
                v.scalar_tensor_tensor(vs[:, :], ssq[:, :], 1.0 / S, vq[:, :], ALU.mult, ALU.add).then_inc(e_vs, 1)

            def softmax_inputs(b):
                dve.wait_ge(e_rs, b + 1)
                for t in range(TT):
                    v.scalar_tensor_tensor(prob[:, t, :], bank[t][:, :], rs[:, t:t + 1], gamma_b[:, :],
                                           ALU.mult, ALU.mult).then_inc(e_scaled, 1)
                settle()
                for t in range(TT):
                    v.tensor_tensor_reduce(out=prob[:, t, :], in0=prob[:, t, :], in1=beta_b[:, :], scale=-1.0,
                                           scalar=3.0e38, op0=ALU.add, op1=ALU.min,
                                           accum_out=nmax[:, t:t + 1]).then_inc(e_logit, 1)

            def add_attention(b):
                dve.wait_ge(e_exp, TT * b + TT)
                v.reciprocal(coef[:, :], esum[:, :])
                settle()
                v.tensor_scalar(coef[:, :], coef[:, :], gt[:, 0:1], None, ALU.mult)
                settle()
                for t in range(TT):
                    v.scalar_tensor_tensor(tile_of(b * TT + t), prob[:, t, :], coef[:, t:t + 1], tile_of(b * TT + t),
                                           ALU.mult, ALU.add)
                settle()

            def row_stats(b):
                for t in range(TT):
                    v.bn_stats(bnh[:, t, :], tile_of(b * TT + t))
                settle()
                for t in range(TT):
                    v.bn_aggr(mvh[:, t, :], bnh[:, t, :])
                settle()
                v.tensor_scalar(vh[:, :], mvh[:, :, 1], EPS_LN, None, ALU.add).then_inc(e_vh, 1)

            def normalise(b):
                dve.wait_ge(e_rh, b + 1)
                if not isinstance(b, int) or b > 0:
                    dve.wait_ge(p_hT, KD * b)
                    dve.wait_ge(st_h, 16 * b)
                for t in range(TT):
                    last = v.tensor_scalar(h[:, t, :], tile_of(b * TT + t), mvh[:, t, 0:1], rh[:, t:t + 1],
                                           ALU.subtract, ALU.mult)
                last.then_inc(e_h, 1)

            def rows_lower(f):
                for k in range(KD):
                    dve.wait_ge(e_hi, KD * f + k + 1)
                    v.tensor_tensor(hT[1][:, k, :], bank[HT_BANK[k]][:, :], hT[0][:, k, :].bitcast(F32), ALU.subtract).then_inc(e_hT, 1)

            def take_logits(f):
                dve.wait_ge(p_z, f + 1)
                zt = z[:, :, f * TT:(f + 1) * TT] if isinstance(f, int) else z[:, :, bass.ds(f * TT, TT)]
                v.tensor_tensor(zt.rearrange("p e t -> p t e"), zps[:, :, 0:E], bc(eb[:, :].unsqueeze(1), [P, TT, E]), ALU.add).then_inc(e_z, 1)

            def gate(f, half):
                dve.wait_ge(e_th, 2 * f + half + 1)
                v.scalar_tensor_tensor(th[:, half, :], th[:, half, :], 1.0, bank[X2_BANK[half]][:, :], ALU.add, ALU.mult).then_inc(e_u, 1)
                settle()
                dve.wait_ge(p_x1, 2 * f + half + 1)
                v.scalar_tensor_tensor(gf[:, half, :], th[:, half, :], 0.5, bank[X1_BANK[half]][:, :], ALU.mult, ALU.mult).then_inc(e_g, 1)

            def gate_lower(f, half):
                dve.wait_ge(e_ghi, 2 * f + half + 1)
                v.tensor_tensor(gT[1][:, half, :], gf[:, half, :], gT[0][:, half, :].bitcast(F32), ALU.subtract).then_inc(e_glo, 1)

            def add_shared(f, t):
                dve.wait_ge(p_y, TT * f + t + 1)
                v.scalar_tensor_tensor(tile_of(f * TT + t), bank[Y_BANK[t]][:, :], gt[:, 1:2], tile_of(f * TT + t),
                                       ALU.mult, ALU.add).then_inc(e_y, 1)

            dve.wait_ge(ld_x[0], 16)
            x_stats(0)
            centre_keys(0)
            dve.wait_ge(c_iota, 7)
            v.tensor_copy(pref[:, :, :], prefi[:, :, :])
            v.tensor_copy(row_f[:, :], row_i[:, :])
            v.tensor_copy(tile_f[:, :], tile_i[:, :])
            v.memset(nofirst[:, :, :, :], 1.0)
            settle()
            v.memset(nofirst[:, :, :, 0:1], 0.0)
            dve.wait_ge(ld_rows, 16 * 6)
            dve.wait_ge(c_tanh, 1)
            score_variance(0)
            softmax_inputs(0)
            dve.wait_ge(c_gw, 2)
            v.tensor_tensor(gw[1][:, :, :], gw_raw[:, :, :], gw[0][:, :, :].bitcast(F32), ALU.subtract).then_inc(c_gw, 1)
            add_attention(0)
            row_stats(0)
            centre_keys(1)
            for b in range(1, NB):
                dve.wait_ge(ld_x[b], 16)
            x_stats(1)
            normalise(0)
            score_variance(1)
            rows_lower(0)
            take_logits(0)
            with dve.Fori(2, NB) as b:
                softmax_inputs(b - 1)
                gate(b - 2, 0)
                add_attention(b - 1)
                row_stats(b - 1)
                gate_lower(b - 2, 0)
                gate(b - 2, 1)
                normalise(b - 1)
                gate_lower(b - 2, 1)
                x_stats(b)
                rows_lower(b - 1)
                add_shared(b - 2, 0)
                centre_keys(b)
                take_logits(b - 1)
                add_shared(b - 2, 1)
                add_shared(b - 2, 2)
                add_shared(b - 2, 3)
                score_variance(b)
            softmax_inputs(NB - 1)
            gate(NB - 2, 0)
            add_attention(NB - 1)
            row_stats(NB - 1)
            gate_lower(NB - 2, 0)
            gate(NB - 2, 1)
            normalise(NB - 1)
            gate_lower(NB - 2, 1)
            rows_lower(NB - 1)
            add_shared(NB - 2, 0)
            take_logits(NB - 1)
            for t in range(1, TT):
                add_shared(NB - 2, t)

            settle()
            v.tensor_scalar(signs[:, :, :], z[:, :, :].bitcast(I32), 31, -2 ** 31, ALU.arith_shift_right, ALU.bitwise_or)
            settle()
            v.tensor_tensor(ordered[:, :, :], z[:, :, :].bitcast(I32), signs[:, :, :], ALU.bitwise_xor)

            def per_token(ap):
                return bc(ap.unsqueeze(1), [P, E, NT])

            def choose(src, dst):
                v.tensor_reduce(m1[:, :], src[:, :, :].rearrange("p e t -> p t e"), AX.X, ALU.max)
                settle()
                v.tensor_tensor(eq[:, :, :], src[:, :, :], per_token(m1[:, :]), ALU.is_equal)
                settle()
                v.tensor_tensor(key[:, :, :], eq[:, :, :], bc(pref[:, :, :], [P, E, NT]), ALU.mult)
                settle()
                v.tensor_reduce(m1[:, :], key[:, :, :].rearrange("p e t -> p t e"), AX.X, ALU.max)
                settle()
                v.tensor_tensor(dst, key[:, :, :], per_token(m1[:, :]), ALU.is_equal)
                settle()

            choose(z, one[:, 0, :, :])
            v.scalar_tensor_tensor(z2[:, :, :], one[:, 0, :, :], -3.0e38, z[:, :, :], ALU.mult, ALU.add)
            settle()
            choose(z2, one[:, 1, :, :])
            v.tensor_tensor(mask[:, :, :], one[:, 0, :, :], one[:, 1, :, :], ALU.add).then_inc(r_one, 1)
            settle()
            v.tensor_tensor(plane[:, :, :, :].rearrange("p l e t -> p l (e t)"),
                            ordered[:, :, :].bitcast(U8).rearrange("p e (t l) -> p l (e t)", l=LEVELS),
                            bc(mask[:, :, :].rearrange("p e t -> p (e t)").unsqueeze(1), [P, LEVELS, E * NT]), ALU.mult)
            settle()
            for half in range(2):
                gate(NB - 1, half)
                gate_lower(NB - 1, half)

            def per_expert(ap):
                return bc(ap.unsqueeze(2), [P, E, NT])

            def find_digit(r, scores, thresholds, step):
                for half in range(2):
                    ts = slice(half * NT // 2, (half + 1) * NT // 2)
                    v.tensor_tensor(hit[:, :, :, ts], bc(scores[:, :, ts].unsqueeze(2), [P, E, CAND, NT // 2]),
                                    bc(thresholds[:, :, ts].unsqueeze(1), [P, E, CAND, NT // 2]), ALU.is_ge).then_inc(r_hit, 1)
                if 1 <= r <= TT:
                    add_shared(NB - 1, r - 1)
                dve.wait_ge(r_cnt, r + 1)
                v.tensor_scalar(reach[:, :, :].rearrange("p e c -> p (e c)"), counts, float(CAP), float(step), ALU.is_ge, ALU.mult)
                settle()
                v.tensor_reduce(digit[:, :], reach[:, :, :], AX.X, ALU.add)
                settle()

            for l in range(LEVELS):
                if l == 0:
                    scores = plane[:, LEVELS - 1, :, :]
                else:
                    v.scalar_tensor_tensor(rest[:, :, :], above_by[:, :, :], 512.0, plane[:, LEVELS - 1 - l, :, :], ALU.mult, ALU.add)
                    settle()
                    scores = rest[:, :, :]
                find_digit(2 * l, scores, high, NIBBLE)
                v.tensor_tensor(rest[:, :, :], scores, per_expert(digit[:, :]), ALU.subtract)
                settle()
                find_digit(2 * l + 1, rest[:, :, :], low, 1)
                if l < LEVELS - 1:
                    v.tensor_tensor(above_by[:, :, :], rest[:, :, :], per_expert(digit[:, :]), ALU.subtract)
                    settle()
            v.tensor_tensor(flags[:, 0, :, :], rest[:, :, :], per_expert(digit[:, :]), ALU.is_gt)
            v.tensor_tensor(flags[:, 1, :, :], rest[:, :, :], per_expert(digit[:, :]), ALU.is_equal).then_inc(r_flags, 1)

            def flat(ap):
                return ap.rearrange("p a e t -> p (a e t)")

            dve.wait_ge(r_flagsP, 1)
            v.tensor_tensor_scan(flat(cum[:, :, :, :]), flat(nofirst[:, :, :, :]), total_ps, 0.0, ALU.mult, ALU.add)
            settle()
            v.tensor_tensor(flat(rank[:, :, :, :]), flat(cum[:, :, :, :]), prefix_ps, ALU.add)
            v.tensor_scalar(room[:, :], cum[:, 0, :, NT - 1], -1.0, float(CAP), ALU.mult, ALU.add)
            settle()
            v.tensor_tensor(before[:, :, :], rank[:, 1, :, :], per_expert(room[:, :]), ALU.min)
            v.tensor_tensor(fits[:, :, :], rank[:, 1, :, :], per_expert(room[:, :]), ALU.is_lt)
            settle()
            v.tensor_tensor(slot[:, :, :], rank[:, 0, :, :], before[:, :, :], ALU.add)
            v.tensor_tensor(fits[:, :, :], fits[:, :, :], flags[:, 1, :, :], ALU.mult)
            settle()
            v.tensor_scalar(slf[:, :, :], slot[:, :, :], P - 1, None, ALU.bitwise_and)
            v.tensor_scalar(slg[:, :, :], slot[:, :, :], 7, None, ALU.logical_shift_right)
            v.tensor_tensor(kept[:, :, :], fits[:, :, :], flags[:, 0, :, :], ALU.add)
            settle()
            v.scalar_tensor_tensor(row1[:, :, :], slf[:, :, :], 1.0, kept[:, :, :], ALU.add, ALU.mult)
            v.tensor_copy(slgf[:, :, :], slg[:, :, :])
            settle()
            v.tensor_tensor(rowc[:, :, :, :], one[:, :, :, :], bc(row1[:, :, :].unsqueeze(1), [P, 2, E, NT]), ALU.mult)
            v.tensor_tensor(ing[:, :, :], bc(slgf[:, :, :].rearrange("p e t -> p (e t)").unsqueeze(1), [P, GE, E * NT]),
                            group[:, :, :], ALU.is_equal)
            settle()
            v.tensor_reduce(srow[:, :, :], rowc[:, :, :, :].rearrange("p c e t -> p c t e"), AX.X, ALU.max)
            dve.wait_ge(r_told, 1)
            v.tensor_tensor(place[:, :, :, :], bc(told[:, :, :].unsqueeze(2), [P, 2 * NV, GE, E * NT]),
                            bc(ing[:, :, :].unsqueeze(1), [P, 2 * NV, GE, E * NT]), ALU.mult)
            settle()
            for c in range(2):
                v.tensor_tensor(hot[:, c, :, :], bc(srow[:, c:c + 1, :], [P, P, NT]), iota_s[:, :, :],
                                ALU.is_equal).then_inc(r_hot, 1)
            dve.wait_ge(r_slot, 1)
            v.tensor_copy(slots[:, :, :].rearrange("p n g -> p (n g)"), slots_ps)
            settle()
            v.scalar_tensor_tensor(tok[:, :], slots[:, 0, :], float(P), slots[:, 1, :], ALU.mult, ALU.add)
            v.tensor_tensor(wsum[:, :], slots[:, 2, :], slots[:, 3, :], ALU.add)
            settle()
            v.tensor_tensor(wslot[:, :], wsum[:, :], slots[:, 4, :], ALU.add).then_inc(r_idx, 1)

            def gathered_lower(e):
                for k in range(KD):
                    dve.wait_ge(f_hi, KD * e + k + 1)
                    v.tensor_tensor(hgT[1][:, k, :], bank[k][:, 0:CAP], hgT[0][:, k, :].bitcast(F32), ALU.subtract).then_inc(f_hgT, 1)

            def lower_w1(n, w1, k):
                dve.wait_ge(w1_hi, W1N * n + k + 1)
                v.tensor_tensor(w1[1][:, k, :], w1_raw[:, k, :], w1[0][:, k, :].bitcast(F32), ALU.subtract).then_inc(w1_lo, 1)

            def lower_w2(n, w2, k):
                dve.wait_ge(w2_hi, W2N * n + k + 1)
                v.tensor_tensor(w2[1][:, k, :], w2_raw[:, k, :], w2[0][:, k, :].bitcast(F32), ALU.subtract).then_inc(w2_lo, 1)

            def routed_gate(e, half):
                dve.wait_ge(f_th, 2 * e + half + 1)
                v.scalar_tensor_tensor(th[:, half, 0:CAP], th[:, half, 0:CAP], 1.0, bank[4 + 2 * half][:, 0:CAP],
                                       ALU.add, ALU.mult)
                settle()
                dve.wait_ge(q_x1, 2 * e + half + 1)
                v.scalar_tensor_tensor(gf[:, half, 0:CAP], th[:, half, 0:CAP], 0.5, bank[5 + 2 * half][:, 0:CAP],
                                       ALU.mult, ALU.mult).then_inc(f_g, 1)

            def routed_gate_lower(e, half):
                dve.wait_ge(f_ghi, 2 * e + half + 1)
                v.tensor_tensor(gT[1][:, half, 0:CAP], gf[:, half, 0:CAP], gT[0][:, half, 0:CAP].bitcast(F32),
                                ALU.subtract).then_inc(f_glo, 1)

            def expert(e, par):
                last = isinstance(e, int) and e == E - 1
                gathered_lower(e)
                if not last:
                    for k in range(KD - 1):
                        lower_w1(e + 2, w1r[1 - par], k)
                routed_gate(e, 0)
                if not last:
                    lower_w1(e + 2, w1r[1 - par], KD - 1)
                routed_gate_lower(e, 0)
                routed_gate(e, 1)
                if not last:
                    lower_w2(e + 2, w2r[1 - par], 0)
                routed_gate_lower(e, 1)
                if not last:
                    lower_w2(e + 2, w2r[1 - par], 1)

            dve.wait_ge(w2_lo, 2 * W2N)
            expert(0, 0)
            with dve.Fori(1, E - 2, 2) as e:
                expert(e, 1)
                expert(e + 1, 0)
            expert(E - 2, 1)
            expert(E - 1, 0)


_INS = ["x", "ctx_512", "g_xattn", "g_ffn", "L0_xattn_W_k", "L0_xattn_b_k", "L0_xattn_ln_gamma",
        "L0_xattn_ln_beta", "L0_ffn_gate_w", "L0_ffn_expert_bias", "L0_ffn_shared_w1",
        "L0_ffn_shared_w2", "L0_ffn_routed_w1", "L0_ffn_routed_w2"]


def kernel(**inputs):
    import concourse.bacc as bacc
    from concourse.bass_utils import run_bass_kernel_spmd

    nc = bacc.Bacc("TRN2", target_bir_lowering=False, num_devices=1)
    arrays, args = {}, []
    for name in _INS:
        a = np.ascontiguousarray(inputs[name])
        arrays[f"in_{name}"] = a
        args.append(nc.dram_tensor(f"in_{name}", a.shape, mybir.dt.from_np(a.dtype), kind="ExternalInput").ap())
    args.append(nc.dram_tensor("out_0", (NB, S, D), F32, kind="ExternalOutput").ap())
    build(nc, *args)
    r = run_bass_kernel_spmd(nc, [arrays], core_ids=[0])
    return r.results[0]["out_0"]
```

```python
from contextlib import ExitStack

import numpy as np
import concourse.bass as bass
from concourse import mybir

F32 = mybir.dt.float32
F32R = mybir.dt.float32r
BF16 = mybir.dt.bfloat16
I32 = mybir.dt.int32
U32 = mybir.dt.uint32
U8 = mybir.dt.uint8
ALU = mybir.AluOpType
ACT = mybir.ActivationFunctionType
AX = mybir.AxisListType

P = 128
NB = 4
S = 512
D = 512
C = 128
T = NB * S
TT = S // P
NT = T // P
KD = D // P
F = 256
E = 7
CAP = T // E
GE = -(-CAP // P)
GSZ = [min(P, CAP - g * P) for g in range(GE)]
SIM_SCALE2 = 512.0
EPS_SIM = 1e-6
EPS_LN = 1e-5
LEVELS = 4
NIBBLE = 16
CAND = NIBBLE - 1
ROUNDS = 2 * LEVELS
GATE_ROUNDS = 4
W1N, W2N = KD, 2
NV = 5


def build(nc, x, ctx_in, g_x, g_f, W_k, b_k, gamma, beta, gate_w, ebias, sw1, sw2, rw1, rw2, out):
    with ExitStack() as stack:
        def alloc(where, name, shape, dt=F32):
            return where.enter_context(nc.sbuf_tensor(name, shape, dt))

        def sb(name, shape, dt=F32):
            return alloc(stack, name, shape, dt)

        def pair(where, name, shape):
            return [alloc(where, f"{name}_{part}", shape, F32R) for part in ("hi", "lo")]

        def sem(name):
            return stack.enter_context(nc.semaphore(name))

        bank = [stack.enter_context(nc.psum_tensor(f"bank{i}", [P, 512], F32)) for i in range(8)]
        h_dram = nc.dram_tensor("h_rows", [T, D], F32, kind="Internal").ap()

        ident = sb("ident", [P, P])
        later = sb("later", [P, P], BF16)
        ones = sb("ones", [P, P], BF16)
        minus = sb("minus", [P, P], BF16)
        WkT = sb("WkT", [P, C])
        bk_col = sb("bk_col", [P, 1])
        gates = sb("gates", [P, 2])
        gt = sb("gt", [P, 2])
        eb = sb("eb", [P, E])
        w1_raw = sb("w1_raw", [P, KD, 2 * F])
        w2_raw = sb("w2_raw", [P, 2, D])
        w1s = pair(stack, "w1s", [P, KD, 2 * F])
        w2s = pair(stack, "w2s", [P, 2, D])
        w1r = [pair(stack, "w1r0", [P, KD, 2 * F])]
        w2r = [pair(stack, "w2r0", [P, 2, D])]
        xs = sb("xs", [P, NT, D])
        hT = pair(stack, "hT", [P, KD, S])
        th = sb("th", [P, 2, S])
        gf = sb("gf", [P, 2, S])
        gT = pair(stack, "gT", [P, 2, S])
        z = sb("z", [P, E, NT])
        z2 = sb("z2", [P, E, NT])
        m1 = sb("m1", [P, NT])
        eq = sb("eq", [P, E, NT])
        key = sb("key", [P, E, NT])
        one = sb("one", [P, 2, E, NT])
        mask = sb("mask", [P, E, NT])
        pref = sb("pref", [P, E, 1])
        prefi = sb("prefi", [P, E, 1], I32)
        signs = sb("signs", [P, E, NT], I32)
        ordered = sb("ordered", [P, E, NT], I32)
        plane = sb("plane", [P, LEVELS, E, NT], BF16)
        wt = sb("wt", [P, E, NT])
        wpart = sb("wpart", [P, E, NT], BF16)
        high = sb("high", [P, CAND, NT], BF16)
        low = sb("low", [P, CAND, NT], BF16)
        rest = sb("rest", [P, E, NT], BF16)
        above_by = sb("above_by", [P, E, NT], BF16)
        reach = sb("reach", [P, E, CAND])
        digit = sb("digit", [P, E])
        flags = sb("flags", [P, 2, E, NT], BF16)
        cum = sb("cum", [P, 2, E, NT])
        rank = sb("rank", [P, 2, E, NT])
        room = sb("room", [P, E])
        nofirst = sb("nofirst", [P, 2, E, NT])
        fits = sb("fits", [P, E, NT])
        before = sb("before", [P, E, NT])
        kept = sb("kept", [P, E, NT])
        slot = sb("slot", [P, E, NT], I32)
        slf = sb("slf", [P, E, NT], I32)
        slg = sb("slg", [P, E, NT], I32)
        slgf = sb("slgf", [P, E, NT], BF16)
        group = sb("group", [P, GE, E * NT], BF16)
        row1 = sb("row1", [P, E, NT])
        srow = sb("srow", [P, 2, NT], BF16)
        iota_s = sb("iota_s", [P, P, NT], BF16)
        row_i = sb("row_i", [P, 1], I32)
        row_f = sb("row_f", [P, 1])
        tile_i = sb("tile_i", [P, NT], I32)
        tile_f = sb("tile_f", [P, NT])
        slots = sb("slots", [P, NV, GE * E])
        tok = sb("tok", [P, GE * E], I32)
        wsum = sb("wsum", [P, GE * E])
        wslot = sb("wslot", [P, GE * E])
        kvsum = sb("kvsum", [P, 1])
        unused = sb("unused", [P, TT, S], BF16)
        ssq = sb("ssq", [P, TT])
        bnx = sb("bnx", [P, TT, 6])
        mvx = sb("mvx", [P, TT, 2])
        vq = sb("vq", [P, NB * TT])
        vs = sb("vs", [P, TT])
        rs = sb("rs", [P, TT])
        mhalf = sb("mhalf", [P, TT])
        nmax = sb("nmax", [P, TT])
        esum = sb("esum", [P, TT])
        coef = sb("coef", [P, TT])
        bnh = sb("bnh", [P, TT, 6])
        mvh = sb("mvh", [P, TT, 2])
        vh = sb("vh", [P, TT])
        rh = sb("rh", [P, TT])

        with ExitStack() as early:
            xb = alloc(early, "xb", [P, TT, D])
            prob = alloc(early, "prob", [P, TT, S])
            ctxb = alloc(early, "ctxb", [P, TT, C])
            gamma_b = alloc(early, "gamma_b", [P, S])
            beta_b = alloc(early, "beta_b", [P, S])
            h = alloc(early, "h", [P, TT, D])
            ctxT = alloc(early, "ctxT", [P, S])
            kvT = alloc(early, "kvT", [P, S])
            kvcT = alloc(early, "kvcT", [P, S])
            kvc = alloc(early, "kvc", [P, TT, C])
            xT = alloc(early, "xT", [P, TT, S])
            outT = alloc(early, "outT", [P, S])
            Wk_rows = alloc(early, "Wk_rows", [P, C])
            gw_raw = alloc(early, "gw_raw", [P, KD, P])
            gw = pair(early, "gw", [P, KD, P])
            zT = alloc(early, "zT", [P, S])
        with ExitStack() as late:
            w1r.append(pair(late, "w1r1", [P, KD, 2 * F]))
            w2r.append(pair(late, "w2r1", [P, 2, D]))
            xg = [alloc(late, f"xg{i}", [P, GE, D]) for i in range(2)]
            yr = [alloc(late, f"yr{i}", [P, GE, D]) for i in range(2)]
            hgT = pair(late, "hgT", [P, KD, CAP])
        with ExitStack() as between:
            hot = alloc(between, "hot", [P, 2, P, NT], BF16)
            place = alloc(between, "place", [P, 2 * NV, GE, E * NT], BF16)
            hit = alloc(between, "hit", [P, E, CAND, NT], BF16)
            rowc = alloc(between, "rowc", [P, 2, E, NT])
            ing = alloc(between, "ing", [P, GE, E * NT], BF16)
            told = alloc(between, "told", [P, 2 * NV, E * NT], BF16)

        block = stack.enter_context(nc.Block())

        ld_wk, ld_bk, ld_rows, ld_ctx, ld_xb, ld_w1, ld_w2 = (sem(n) for n in
            ("ld_wk", "ld_bk", "ld_rows", "ld_ctx", "ld_xb", "ld_w1", "ld_w2"))
        ld_x = [sem(f"ld_x{i}") for i in range(NB)]
        st_h = sem("st_h")
        st_out = sem("st_out")
        gath = [sem(f"gath{i}") for i in range(2)]
        scat = [sem(f"scat{i}") for i in range(2)]
        y_landed = sem("y_landed")
        c_pool, c_iota, c_wk, c_wkT, c_tanh, c_gw = (sem(n) for n in ("c_pool", "c_iota", "c_wk", "c_wkT", "c_tanh", "c_gw"))
        w1_hi, w1_lo, w2_hi, w2_lo = (sem(n) for n in ("w1_hi", "w1_lo", "w2_hi", "w2_lo"))
        p_ctxT, p_xT, p_kvT, p_kvc, p_outT, p_S = (sem(n) for n in
            ("p_ctxT", "p_xT", "p_kvT", "p_kvc", "p_outT", "p_S"))
        e_ctxT, e_xT, e_kvT, e_kvcT, e_kvc, e_outT = (sem(n) for n in
            ("e_ctxT", "e_xT", "e_kvT", "e_kvcT", "e_kvc", "e_outT"))
        e_stats, e_ssq, e_vs, e_rs, e_scaled, e_logit, e_exp, e_vh, e_rh, e_h = (sem(n) for n in
            ("e_stats", "e_ssq", "e_vs", "e_rs", "e_scaled", "e_logit", "e_exp", "e_vh", "e_rh", "e_h"))
        p_hT, p_zT, p_z, p_x2, p_x1, p_y = (sem(n) for n in ("p_hT", "p_zT", "p_z", "p_x2", "p_x1", "p_y"))
        e_hi, e_hT, e_zT, e_z, e_th, e_u, e_g, e_ghi, e_glo, e_y = (sem(n) for n in
            ("e_hi", "e_hT", "e_zT", "e_z", "e_th", "e_u", "e_g", "e_ghi", "e_glo", "e_y"))
        r_sig, r_one, r_told, r_hit, r_cnt, r_flags, r_flagsP, r_hot, r_slot, r_idx, r_weight = (sem(n) for n in
            ("r_sig", "r_one", "r_told", "r_hit", "r_cnt", "r_flags", "r_flagsP", "r_hot", "r_slot", "r_idx", "r_weight"))
        q_hgT, q_x2, q_x1, q_y = (sem(n) for n in ("q_hgT", "q_x2", "q_x1", "q_y"))
        f_hi, f_hgT, f_th, f_g, f_ghi, f_glo, f_y = (sem(n) for n in
            ("f_hi", "f_hgT", "f_th", "f_g", "f_ghi", "f_glo", "f_y"))

        def bc(ap, shape):
            return ap.broadcast_to(shape)

        counts = bank[7][:, 0:E * CAND]
        zps = bank[7][:, :].rearrange("p (t e) -> p t e", e=P)
        total_ps = bank[7][:, 0:2 * E * NT]
        prefix_ps = bank[7][:, 2 * E * NT:4 * E * NT]
        slots_ps = bank[0][:, 0:NV * GE * E]

        HT_BANK = (4, 5, 6, 4)
        X2_BANK, X1_BANK = (5, 6), (4, 5)
        Y_BANK = (6, 4, 5, 6)

        @block.sync
        def _(sp):
            def row(v, n):
                return v.rearrange("(o n) -> o n", o=1).broadcast_to([P, n])

            sp.dma_start(ctxb[:, :, :], ctx_in[0].rearrange("(t p) c -> p t c", p=P)).then_inc(ld_ctx, 16)
            sp.dma_start(Wk_rows[:, :], W_k).then_inc(ld_wk, 16)
            sp.dma_start(xb[:, :, :], x[0].rearrange("(t p) d -> p t d", p=P)).then_inc(ld_xb, 16)
            sp.dma_start(bk_col[:, :], b_k.rearrange("(p o) -> p o", o=1)).then_inc(ld_bk, 16)
            h_rows = h_dram.rearrange("(b t p) d -> b p t d", p=P, t=TT)
            out_rows = out.rearrange("b (t p) d -> b p t d", p=P)
            ctx_rows = ctx_in.rearrange("b (t p) c -> b p t c", p=P)
            x_rows = x.rearrange("b (t p) d -> b p t d", p=P)

            def load_x(b):
                sp.dma_start(xs[:, b * TT:(b + 1) * TT, :], x_rows[b]).then_inc(ld_x[b], 16)

            sp.dma_start(w1_raw[:, :, :], sw1[0].rearrange("(k p) f -> p k f", p=P)).then_inc(ld_w1, 16)
            sp.dma_start(w2_raw[:, :, :], sw2[0].rearrange("(k p) d -> p k d", p=P)).then_inc(ld_w2, 16)
            load_x(1)
            sp.wait_ge(p_ctxT, 1)
            sp.dma_start(ctxb[:, :, :], ctx_rows[1]).then_inc(ld_ctx, 16)
            sp.dma_start(gates[:, 0:1], row(g_x, 1)).then_inc(ld_rows, 16)
            sp.dma_start(gates[:, 1:2], row(g_f, 1)).then_inc(ld_rows, 16)
            sp.dma_start(gamma_b[:, :], row(gamma, S)).then_inc(ld_rows, 16)
            sp.dma_start(beta_b[:, :], row(beta, S)).then_inc(ld_rows, 16)
            sp.dma_start(eb[:, :], row(ebias, E)).then_inc(ld_rows, 16)
            sp.wait_ge(c_gw, 1)
            sp.dma_start(gw_raw[:, :, 0:E], gate_w.rearrange("(k p) e -> p k e", p=P)).then_inc(ld_rows, 16)
            sp.wait_ge(p_xT, TT)
            sp.wait_ge(e_stats, 1)
            sp.dma_start(xb[:, :, :], x_rows[1]).then_inc(ld_xb, 16)
            for b in (0, 2, 3):
                load_x(b)
            sp.wait_ge(e_h, 1)
            sp.dma_start(h_rows[0], h[:, :, :]).then_inc(st_h, 16)
            with sp.Fori(1, NB - 1) as b:
                sp.wait_ge(p_ctxT, b + 1)
                sp.dma_start(ctxb[:, :, :], ctx_rows[bass.ds(b + 1, 1), :, :, :].rearrange("o p t c -> (o p) t c")).then_inc(ld_ctx, 16)
                sp.wait_ge(p_xT, TT * b + TT)
                sp.dma_start(xb[:, :, :], x_rows[bass.ds(b + 1, 1), :, :, :].rearrange("o p t d -> (o p) t d")).then_inc(ld_xb, 16)
                sp.wait_ge(e_h, b + 1)
                sp.dma_start(h_rows[bass.ds(b, 1), :, :, :].rearrange("o p t d -> (o p) t d"), h[:, :, :]).then_inc(st_h, 16)
            sp.wait_ge(w1_lo, W1N)
            sp.wait_ge(w2_lo, W2N)
            sp.dma_start(w1_raw[:, :, :], rw1[0].rearrange("(k p) f -> p k f", p=P)).then_inc(ld_w1, 16)
            sp.dma_start(w2_raw[:, :, :], rw2[0].rearrange("(k p) d -> p k d", p=P)).then_inc(ld_w2, 16)
            sp.wait_ge(e_h, NB)
            sp.dma_start(h_rows[NB - 1], h[:, :, :]).then_inc(st_h, 16)
            with sp.Fori(0, NB) as b:
                sp.wait_ge(e_y, TT * b + TT)
                sp.dma_start(out_rows[bass.ds(b, 1), :, :, :].rearrange("o p t d -> (o p) t d"),
                             xs[:, bass.ds(b * TT, TT), :]).then_inc(st_out, 16)
            w1_rows = rw1.rearrange("e (k p) f -> e p k f", p=P)
            w2_rows = rw2.rearrange("e (k p) d -> e p k d", p=P)
            with sp.Fori(1, E) as e:
                sp.wait_ge(w1_lo, W1N * e + W1N)
                sp.dma_start(w1_raw[:, :, :], w1_rows[bass.ds(e, 1), :, :, :].rearrange("o p k f -> (o p) k f")).then_inc(ld_w1, 16)
                sp.wait_ge(w2_lo, W2N * e + W2N)
                sp.dma_start(w2_raw[:, :, :], w2_rows[bass.ds(e, 1), :, :, :].rearrange("o p k d -> (o p) k d")).then_inc(ld_w2, 16)

        @block.tensor
        def _(pe):
            def transpose(out_ap, in_ap, n=P):
                return nc.tensor.transpose(out_ap, in_ap, ident[0:n, 0:n])

            def product(out_ap, pieces, first=True, final=True):
                todo = [(w[i], m[j]) for w, m in pieces for i, j in ((0, 0), (0, 1), (1, 0))]
                for n, (w, m) in enumerate(todo):
                    last = nc.tensor.matmul(out_ap, w, m, start=first and n == 0, stop=final and n == len(todo) - 1)
                return last

            def both(p, *at):
                return p[0][at], p[1][at]

            A = slice(None)

            def front_bank(b, i):
                return bank[4 + i if isinstance(b, int) and b == 1 else i]

            def scaled(b, i):
                if not isinstance(b, int) or b > 1:
                    pe.wait_ge(e_scaled, TT * b - 3 + i)

            def context(b):
                pe.wait_ge(ld_ctx, 16 * b + 16)
                scaled(b, 0)
                for t in range(TT):
                    last = transpose(front_bank(b, 0)[:, t * P:(t + 1) * P], ctxb[:, t, :])
                last.then_inc(p_ctxT, 1)

            def x_cols(b, j, i):
                for t in range(TT):
                    last = transpose(front_bank(b, i)[:, t * P:(t + 1) * P], xb[:, t, j * P:(j + 1) * P])
                last.then_inc(p_xT, 1)

            def first_x(b):
                pe.wait_ge(ld_xb, 16 * b + 16)
                scaled(b, 1)
                x_cols(b, 0, 1)

            def keys(b):
                pe.wait_ge(e_ctxT, b + 1)
                scaled(b, 2)
                nc.tensor.matmul(front_bank(b, 2)[:, :], WkT[:, :], ctxT[:, :], start=True, stop=True).then_inc(p_kvT, 1)

            def more_x(b):
                scaled(b, 3)
                x_cols(b, 1, 3)
                x_cols(b, 2, 0)

            def keys_back(b):
                pe.wait_ge(e_kvcT, b + 1)
                pe.wait_ge(e_xT, TT * b + 1)
                for t in range(TT):
                    last = transpose(front_bank(b, 1)[:, t * C:(t + 1) * C], kvcT[:, t * P:(t + 1) * P])
                last.then_inc(p_kvc, 1)
                x_cols(b, 3, 2)

            def attend(b):
                pe.wait_ge(e_kvc, b + 1)
                for j in range(TT):
                    if j != 1:
                        pe.wait_ge(e_xT, TT * b + max(j, 1) + 1)
                    last = nc.tensor.matmul(front_bank(b, 3)[:, :], kvc[:, j, :], xT[:, j, :], start=j == 0, stop=j == TT - 1)
                last.then_inc(p_outT, 1)

            def scores(b):
                pe.wait_ge(e_outT, b + 1)
                if isinstance(b, int) and b == 1:
                    pe.wait_ge(e_scaled, TT)
                for t in range(TT):
                    nc.tensor.matmul(bank[t][:, :], outT[:, t * P:(t + 1) * P], kvcT[:, :], start=True, stop=True).then_inc(p_S, 1)

            def rows_back(f):
                later = not isinstance(f, int) or f > 0
                pe.wait_ge(e_h, f + 1)
                for k in range(KD):
                    if later and k == 0:
                        pe.wait_ge(e_y, TT * f - 2)
                    if later and k == 1:
                        pe.wait_ge(e_y, TT * f - 1)
                    if later and k == 2:
                        pe.wait_ge(e_y, TT * f)
                    if k == 3:
                        pe.wait_ge(e_hT, KD * f + 1)
                    for t in range(TT):
                        last = transpose(bank[HT_BANK[k]][:, t * P:(t + 1) * P], h[:, t, k * P:(k + 1) * P])
                    last.then_inc(p_hT, 1)
                pe.wait_ge(e_z, f + 1)
                for k in range(KD):
                    pe.wait_ge(e_hT, KD * f + k + 1)
                    done = product(bank[7][:, :], [(both(gw, A, k, A), both(hT, A, k, A))], k == 0, k == KD - 1)
                done.then_inc(p_zT, 1)

            def logits(f):
                pe.wait_ge(e_zT, f + 1)
                for t in range(TT):
                    last = transpose(zps[:, t, :], zT[:, t * P:(t + 1) * P])
                last.then_inc(p_z, 1)

            def up(f, half, part):
                if half == 1 and part == 1:
                    pe.wait_ge(e_u, 2 * f + 1)
                bk, done = (X2_BANK[half], p_x2) if part == 0 else (X1_BANK[half], p_x1)
                col = slice((1 - part) * F + half * P, (1 - part) * F + half * P + P)
                product(bank[bk][:, :], [(both(w1s, A, k, col), both(hT, A, k, A)) for k in range(KD)]).then_inc(done, 1)

            def down(f, t):
                pe.wait_ge(e_glo, 2 * f + 2)
                if t == 3:
                    pe.wait_ge(e_y, TT * f + 1)
                col = slice(t * P, (t + 1) * P)
                product(bank[Y_BANK[t]][:, :], [(both(gT, A, k, col), both(w2s, A, k, A)) for k in range(2)]).then_inc(p_y, 1)

            pe.wait_ge(c_pool, 4)
            pe.wait_ge(ld_wk, 16)
            transpose(bank[7][:, 0:C], Wk_rows[:, :]).then_inc(c_wk, 1)
            context(0)
            pe.wait_ge(c_wkT, 1)
            for b in range(2):
                if b == 0:
                    keys(0)
                    first_x(0)
                else:
                    context(1)
                    first_x(1)
                    keys(1)
                more_x(b)
                keys_back(b)
                attend(b)
                if b == 0:
                    scores(0)
            pe.wait_ge(c_gw, 3)
            pe.wait_ge(w1_lo, W1N)
            pe.wait_ge(w2_lo, W2N)
            scores(1)
            rows_back(0)
            with pe.Fori(2, NB) as b:
                up(b - 2, 0, 0)
                up(b - 2, 0, 1)
                logits(b - 2)
                context(b)
                first_x(b)
                up(b - 2, 1, 0)
                keys(b)
                up(b - 2, 1, 1)
                more_x(b)
                keys_back(b)
                attend(b)
                scores(b)
                for t in range(TT):
                    down(b - 2, t)
                rows_back(b - 1)
            up(NB - 2, 0, 0)
            up(NB - 2, 0, 1)
            logits(NB - 2)
            up(NB - 2, 1, 0)
            up(NB - 2, 1, 1)
            for t in range(TT):
                down(NB - 2, t)
            rows_back(NB - 1)
            up(NB - 1, 0, 0)
            logits(NB - 1)
            up(NB - 1, 0, 1)
            up(NB - 1, 1, 0)

            def count(r):
                for half in range(2):
                    pe.wait_ge(r_hit, 2 * r + half + 1)
                    for t in range(half * NT // 2, (half + 1) * NT // 2):
                        last = nc.tensor.matmul(counts, ones[:, :], hit[:, :, :, t], start=t == 0, stop=t == NT - 1)
                last.then_inc(r_cnt, 1)

            for r in range(ROUNDS):
                count(r)
                if r == 0:
                    up(NB - 1, 1, 1)
                if r >= GATE_ROUNDS - 1 and r < ROUNDS - 1:
                    down(NB - 1, r - GATE_ROUNDS + 1)
            pe.wait_ge(r_flags, 1)
            both_flags = flags[:, :, :, :].rearrange("p a e t -> p (a e t)")
            nc.tensor.matmul(total_ps, ones[:, :], both_flags, start=True, stop=True)
            nc.tensor.matmul(prefix_ps, later[:, :], both_flags, start=True, stop=True).then_inc(r_flagsP, 1)
            for c in range(2):
                pe.wait_ge(r_hot, c + 1)
                for t in range(NT):
                    last = nc.tensor.matmul(slots_ps, hot[:, c, :, t],
                                            place[:, c * NV:(c + 1) * NV, :, :].rearrange("p n g (e t) -> p (n g e) t", t=NT)[:, :, t],
                                            start=c == 0 and t == 0, stop=c == 1 and t == NT - 1)
            last.then_inc(r_slot, 1)

            def gathered(e, par):
                pe.wait_ge(gath[par], (e - par) * (8 * GE) + 16 * GE)
                for k in range(KD):
                    if not isinstance(e, int) or e > 0:
                        pe.wait_ge(f_hgT, KD * e - KD + k + 1)
                    for g in range(GE):
                        last = transpose(bank[k][:, g * P:g * P + GSZ[g]], xg[par][0:GSZ[g], g, k * P:(k + 1) * P], GSZ[g])
                    last.then_inc(q_hgT, 1)

            def routed_up(e, par):
                pe.wait_ge(f_hgT, KD * e + KD)
                pe.wait_ge(w1_lo, W1N * e + 2 * W1N)
                for half in range(2):
                    for part, (w_col, done) in enumerate(((F, q_x2), (0, q_x1))):
                        bk = 2 * half + part
                        if not isinstance(e, int) or e > 0:
                            pe.wait_ge(f_y, GE * e - GE + bk + 1) if bk < GE else pe.wait_ge(f_g, 2 * e)
                        col = slice(w_col + half * P, w_col + half * P + P)
                        product(bank[4 + bk][:, 0:CAP], [(both(w1r[par], A, k, col), both(hgT, A, k, A)) for k in range(KD)]).then_inc(done, 1)

            def routed_down(e, par):
                pe.wait_ge(f_glo, 2 * e + 2)
                pe.wait_ge(w2_lo, W2N * e + 2 * W2N)
                for g in range(GE):
                    col = slice(g * P, g * P + GSZ[g])
                    product(bank[4 + g][0:GSZ[g], :], [(both(gT, A, k, col), both(w2r[par], A, k, A)) for k in range(2)]).then_inc(q_y, 1)

            pe.wait_ge(e_y, TT * NB)
            gathered(0, 0)
            routed_up(0, 0)
            with pe.Fori(1, E, 2) as e:
                gathered(e, 1)
                routed_down(e - 1, 0)
                routed_up(e, 1)
                gathered(e + 1, 0)
                routed_down(e, 1)
                routed_up(e + 1, 0)
            routed_down(E - 1, 0)

        @block.scalar
        def _(act):
            def copy(dst, src):
                return nc.scalar.activation(dst, src, ACT.Copy)

            def upper_w1(n, w1, k):
                if k == 0:
                    act.wait_ge(ld_w1, 16 * n + 16)
                copy(w1[0][:, k, :], w1_raw[:, k, :]).then_inc(w1_hi, 1)

            def upper_w2(n, w2, k):
                if k == 0:
                    act.wait_ge(ld_w2, 16 * n + 16)
                copy(w2[0][:, k, :], w2_raw[:, k, :]).then_inc(w2_hi, 1)

            def upper_weights(n, w1, w2):
                for k in range(W1N):
                    upper_w1(n, w1, k)
                for k in range(W2N):
                    upper_w2(n, w2, k)

            def front_bank(b, i):
                return bank[4 + i if isinstance(b, int) and b == 1 else i]

            def x_copy(b, j, i):
                act.wait_ge(p_xT, TT * b + j + 1)
                copy(xT[:, j, :], front_bank(b, i)[:, :]).then_inc(e_xT, 1)

            def context_copy(b):
                act.wait_ge(p_ctxT, b + 1)
                copy(ctxT[:, :], front_bank(b, 0)[:, :]).then_inc(e_ctxT, 1)
                if not isinstance(b, int) or b > 0:
                    x_copy(b, 0, 1)

            def keys_copy(b):
                act.wait_ge(p_kvT, b + 1)
                nc.scalar.activation(kvT[:, :], front_bank(b, 2)[:, :], ACT.Identity, bias=bk_col[:, 0:1],
                                     accum_out=kvsum[:, :]).then_inc(e_kvT, 1)
                if isinstance(b, int) and b == 0:
                    x_copy(b, 0, 1)
                x_copy(b, 1, 3)
                x_copy(b, 2, 0)

            def keys_back_copy(b):
                act.wait_ge(p_kvc, b + 1)
                copy(kvc[:, :, :].rearrange("p t c -> p (t c)"), front_bank(b, 1)[:, :]).then_inc(e_kvc, 1)
                x_copy(b, 3, 2)

            def out_copy(b):
                act.wait_ge(p_outT, b + 1)
                copy(outT[:, :], front_bank(b, 3)[:, :]).then_inc(e_outT, 1)

            def squares(b):
                for t in range(TT):
                    act.wait_ge(p_S, TT * b + t + 1)
                    nc.scalar.activation(unused[:, t, :], bank[t][:, :], ACT.Square, accum_out=ssq[:, t:t + 1]).then_inc(e_ssq, 1)

            def exps(b):
                for t in range(TT):
                    act.wait_ge(e_logit, TT * b + t + 1)
                    nc.scalar.activation(prob[:, t, :], prob[:, t, :], ACT.Exp, bias=nmax[:, t:t + 1], scale=-1.0,
                                         accum_out=esum[:, t:t + 1]).then_inc(e_exp, 1)

            def rows_upper(f):
                for k in range(KD):
                    act.wait_ge(p_hT, KD * f + k + 1)
                    copy(hT[0][:, k, :], bank[HT_BANK[k]][:, :]).then_inc(e_hi, 1)
                act.wait_ge(p_zT, f + 1)
                copy(zT[:, :], bank[7][:, :]).then_inc(e_zT, 1)

            def gate_tanh(f, half):
                act.wait_ge(p_x2, 2 * f + half + 1)
                nc.scalar.activation(th[:, half, :], bank[X2_BANK[half]][:, :], ACT.Tanh, scale=0.5).then_inc(e_th, 1)

            def gate_upper(f, half):
                act.wait_ge(e_g, 2 * f + half + 1)
                copy(gT[0][:, half, :], gf[:, half, :]).then_inc(e_ghi, 1)

            act.wait_ge(c_wk, 1)
            copy(WkT[:, :], bank[7][:, 0:C]).then_inc(c_wkT, 1)
            context_copy(0)
            act.wait_ge(ld_bk, 16)
            keys_copy(0)
            keys_back_copy(0)
            upper_weights(0, w1s, w2s)
            out_copy(0)
            act.wait_ge(ld_rows, 16 * 6)
            nc.scalar.activation(gt[:, :], gates[:, :], ACT.Tanh).then_inc(c_tanh, 1)
            squares(0)
            context_copy(1)
            keys_copy(1)
            copy(gw[0][:, :, :], gw_raw[:, :, :]).then_inc(c_gw, 1)
            exps(0)
            keys_back_copy(1)
            out_copy(1)
            act.wait_ge(e_rs, 1)
            squares(1)
            rows_upper(0)
            with act.Fori(2, NB) as b:
                gate_tanh(b - 2, 0)
                exps(b - 1)
                gate_upper(b - 2, 0)
                context_copy(b)
                gate_tanh(b - 2, 1)
                keys_copy(b)
                keys_back_copy(b)
                gate_upper(b - 2, 1)
                out_copy(b)
                squares(b)
                rows_upper(b - 1)
            gate_tanh(NB - 2, 0)
            exps(NB - 1)
            gate_tanh(NB - 2, 1)
            gate_upper(NB - 2, 0)
            gate_upper(NB - 2, 1)
            rows_upper(NB - 1)
            gate_tanh(NB - 1, 0)
            act.wait_ge(e_z, NB + 1)
            nc.scalar.activation(wt[:, :, :].rearrange("p e t -> p (e t)"), z[:, :, :].rearrange("p e t -> p (e t)"),
                                 ACT.Tanh, scale=0.5).then_inc(r_sig, 1)
            gate_upper(NB - 1, 0)
            gate_tanh(NB - 1, 1)
            gate_upper(NB - 1, 1)
            upper_weights(1, w1r[0], w2r[0])

            def gathered_upper(e):
                for k in range(KD):
                    act.wait_ge(q_hgT, KD * e + k + 1)
                    copy(hgT[0][:, k, :], bank[k][:, 0:CAP]).then_inc(f_hi, 1)

            def routed_tanh(e, half):
                act.wait_ge(q_x2, 2 * e + half + 1)
                nc.scalar.activation(th[:, half, 0:CAP], bank[4 + 2 * half][:, 0:CAP], ACT.Tanh, scale=0.5).then_inc(f_th, 1)

            def routed_gate_upper(e, half):
                act.wait_ge(f_g, 2 * e + half + 1)
                copy(gT[0][:, half, 0:CAP], gf[:, half, 0:CAP]).then_inc(f_ghi, 1)

            def scaled(e, par, g):
                if g == 0:
                    act.wait_ge(y_landed, e + 1)
                act.wait_ge(q_y, GE * e + g + 1)
                w = wslot[0:GSZ[g], g * E + e:g * E + e + 1] if isinstance(e, int) else wslot[0:GSZ[g], bass.ds(e + g * E, 1)]
                nc.scalar.activation(yr[par][0:GSZ[g], g, :], bank[4 + g][0:GSZ[g], :], ACT.Copy, scale=w).then_inc(f_y, 1)

            def expert(e, par):
                first, last = isinstance(e, int) and e == 0, isinstance(e, int) and e == E - 1
                w1, w2 = w1r[1 - par], w2r[1 - par]
                gathered_upper(e)
                for g in range(GE):
                    if not last:
                        upper_w1(e + 2, w1, g)
                    if not first:
                        scaled(e - 1, 1 - par, g)
                routed_tanh(e, 0)
                if not last:
                    upper_w1(e + 2, w1, KD - 1)
                routed_gate_upper(e, 0)
                routed_tanh(e, 1)
                if not last:
                    upper_w2(e + 2, w2, 0)
                    upper_w2(e + 2, w2, 1)
                routed_gate_upper(e, 1)

            act.wait_ge(r_weight, 1)
            expert(0, 0)

            with act.Fori(1, E - 2, 2) as e:
                expert(e, 1)
                expert(e + 1, 0)
            expert(E - 2, 1)
            expert(E - 1, 0)
            for g in range(GE):
                scaled(E - 1, 0, g)

        @block.gpsimd
        def _(pool):
            g_ = nc.gpsimd
            g_.memset(ident[:, :], 0.0)
            g_.memset(ones[:, :], 1.0).then_inc(c_pool, 1)
            g_.memset(minus[:, :], -1.0)
            g_.memset(mhalf[:, :], -0.5).then_inc(c_pool, 1)
            g_.memset(gw_raw[:, :, :], 0.0).then_inc(c_gw, 1)
            g_.drain()
            g_.affine_select(out=ident[:, :], in_=ident[:, :], compare_op=ALU.not_equal, fill=1.0, base=0,
                             pattern=[[-1, P]], channel_multiplier=1).then_inc(c_pool, 1)
            g_.affine_select(out=later[:, :], in_=minus[:, :], compare_op=ALU.is_ge, fill=0.0, base=0,
                             pattern=[[-1, P]], channel_multiplier=1).then_inc(c_pool, 1)
            g_.iota(prefi[:, :, 0], [[-1, E]], base=E, channel_multiplier=0).then_inc(c_iota, 1)
            g_.iota(row_i[:, :], [[0, 1]], base=0, channel_multiplier=1).then_inc(c_iota, 1)
            g_.iota(tile_i[:, :], [[1, NT]], base=0, channel_multiplier=0).then_inc(c_iota, 1)
            for step, dst in ((NIBBLE, high), (1, low)):
                g_.iota(dst[:, :, :], [[step, CAND], [0, NT]], base=step, channel_multiplier=0,
                        allow_small_or_imprecise_dtypes=True).then_inc(c_iota, 1)
            g_.iota(group[:, :, :], [[1, GE], [0, E * NT]], base=0, channel_multiplier=0,
                    allow_small_or_imprecise_dtypes=True).then_inc(c_iota, 1)
            g_.iota(iota_s[:, :, :], [[1, P], [0, NT]], base=1, channel_multiplier=0,
                    allow_small_or_imprecise_dtypes=True).then_inc(c_iota, 1)

            def inverse_root_scores(b):
                pool.wait_ge(e_vs, b + 1)
                g_.tensor_tensor(rs[:, :], vs[:, :], mhalf[:, :], ALU.pow).then_inc(e_rs, 1)

            def inverse_root_rows(b):
                pool.wait_ge(e_vh, b + 1)
                g_.tensor_tensor(rh[:, :], vh[:, :], mhalf[:, :], ALU.pow).then_inc(e_rh, 1)

            def lower_weights(n, w1, w2):
                for w, raw, pieces, hi, lo in ((w1, w1_raw, W1N, w1_hi, w1_lo), (w2, w2_raw, W2N, w2_hi, w2_lo)):
                    for k in range(pieces):
                        pool.wait_ge(hi, pieces * n + k + 1)
                        g_.tensor_tensor(w[1][:, k, :], raw[:, k, :], w[0][:, k, :].bitcast(F32), ALU.subtract).then_inc(lo, 1)

            lower_weights(0, w1s, w2s)
            inverse_root_scores(0)
            inverse_root_rows(0)
            with pool.Fori(1, NB) as b:
                inverse_root_scores(b)
                inverse_root_rows(b)

            pool.wait_ge(r_one, 1)
            def tell(n, ap):
                told_n = told[:, :, :].rearrange("p (c n) (e t) -> p n c e t", n=NV, t=NT)[:, n, :, :, :]
                return g_.tensor_tensor(told_n, one[:, :, :, :], ap, ALU.mult)

            tell(0, bc(tile_f[:, :].unsqueeze(1).unsqueeze(1), [P, 2, E, NT]))
            tell(1, bc(row_f[:, :].unsqueeze(1).unsqueeze(1), [P, 2, E, NT]))
            pool.wait_ge(r_sig, 1)
            g_.tensor_scalar(wt[:, :, :], wt[:, :, :], 0.5, 0.5, ALU.mult, ALU.add)
            g_.drain()
            g_.tensor_scalar(wt[:, :, :], wt[:, :, :], gt[:, 1:2], None, ALU.mult)
            g_.drain()
            for i in range(3):
                g_.tensor_copy(wpart[:, :, :], wt[:, :, :])
                g_.drain()
                last = tell(2 + i, bc(wpart[:, :, :].unsqueeze(1), [P, 2, E, NT]))
                g_.tensor_tensor(wt[:, :, :], wt[:, :, :], wpart[:, :, :], ALU.subtract)
                g_.drain()
            last.then_inc(r_told, 1)
            lower_weights(1, w1r[0], w2r[0])

            pool.wait_ge(st_h, 16 * NB)
            pool.wait_ge(r_idx, 1)

            def index(e, g):
                return bass.IndirectOffsetOnAxis(ap=tok[0:GSZ[g], g * E + e:g * E + e + 1].bitcast(U32), axis=0)

            def gather(e):
                for g in range(GE):
                    g_.indirect_dma_start(xg[e % 2][0:GSZ[g], g, :], None, h_dram, index(e, g),
                                          bounds_check=T - 1).then_inc(gath[e % 2], 16)

            rows = out.rearrange("b s d -> (b s) d")
            g_.sem_inc(y_landed, 2)
            gather(0)
            gather(1)
            pool.wait_ge(st_out, 16 * NB)
            for e in range(E):
                if e + 2 < E:
                    pool.wait_ge(q_hgT, KD * e + KD)
                    gather(e + 2)
                if e >= 1:
                    pool.wait_ge(scat[(e - 1) % 2], 16 * GE * ((e - 1) // 2 + 1))
                    g_.sem_inc(y_landed, 1)
                for g in range(GE):
                    pool.wait_ge(f_y, GE * e + g + 1)
                    g_.indirect_dma_start(rows, index(e, g), yr[e % 2][0:GSZ[g], g, :], None, bounds_check=T - 1,
                                          compute_op=ALU.add).then_inc(scat[e % 2], 16)
            for i in range(2):
                pool.wait_ge(scat[i], 16 * GE * len(range(i, E, 2)))

        @block.vector
        def _(dve):
            v = nc.vector

            def settle():
                return v.drain()

            v.sem_inc(e_z, 1)

            def tile_of(t):
                return xs[:, t, :] if isinstance(t, int) else xs[:, bass.ds(t, 1), :].rearrange("p o d -> p (o d)")

            def variances(b):
                return vq[:, b * TT:(b + 1) * TT] if isinstance(b, int) else vq[:, bass.ds(b * TT, TT)]

            def x_stats(b):
                for t in range(TT):
                    first = isinstance(b, int) and b == 0
                    v.bn_stats(bnx[:, t, :], xb[:, t, :] if first else tile_of(b * TT + t))
                settle()
                for t in range(TT):
                    v.bn_aggr(mvx[:, t, :], bnx[:, t, :])
                settle()
                v.tensor_scalar(variances(b), mvx[:, :, 1], EPS_LN, EPS_SIM * SIM_SCALE2, ALU.add, ALU.mult)
                settle()

            def centre_keys(b):
                dve.wait_ge(e_kvT, b + 1)
                v.tensor_scalar(kvsum[:, :], kvsum[:, :], 1.0 / S, None, ALU.mult)
                settle()
                v.tensor_scalar(kvcT[:, :], kvT[:, :], kvsum[:, 0:1], None, ALU.subtract).then_inc(e_kvcT, 1)

            def score_variance(b):
                dve.wait_ge(e_ssq, TT * b + TT)
                v.scalar_tensor_tensor(vs[:, :], ssq[:, :], 1.0 / S, variances(b), ALU.mult, ALU.add).then_inc(e_vs, 1)

            def softmax_inputs(b):
                dve.wait_ge(e_rs, b + 1)
                for t in range(TT):
                    v.scalar_tensor_tensor(prob[:, t, :], bank[t][:, :], rs[:, t:t + 1], gamma_b[:, :],
                                           ALU.mult, ALU.mult).then_inc(e_scaled, 1)
                if isinstance(b, int) and b == 0:
                    centre_keys(1)
                settle()
                for t in range(TT):
                    v.tensor_tensor_reduce(out=prob[:, t, :], in0=prob[:, t, :], in1=beta_b[:, :], scale=-1.0,
                                           scalar=3.0e38, op0=ALU.add, op1=ALU.min,
                                           accum_out=nmax[:, t:t + 1]).then_inc(e_logit, 1)

            def add_attention(b):
                dve.wait_ge(e_exp, TT * b + TT)
                v.reciprocal(coef[:, :], esum[:, :])
                settle()
                v.tensor_scalar(coef[:, :], coef[:, :], gt[:, 0:1], None, ALU.mult)
                settle()
                for t in range(TT):
                    v.scalar_tensor_tensor(tile_of(b * TT + t), prob[:, t, :], coef[:, t:t + 1], tile_of(b * TT + t),
                                           ALU.mult, ALU.add)
                settle()

            def row_stats(b, tiles=range(TT)):
                for t in tiles:
                    v.bn_stats(bnh[:, t, :], tile_of(b * TT + t))
                if TT - 1 in tiles:
                    settle()
                    for t in range(TT):
                        v.bn_aggr(mvh[:, t, :], bnh[:, t, :])
                    settle()
                    v.tensor_scalar(vh[:, :], mvh[:, :, 1], EPS_LN, None, ALU.add).then_inc(e_vh, 1)

            def normalise(b):
                dve.wait_ge(e_rh, b + 1)
                if not isinstance(b, int) or b > 0:
                    dve.wait_ge(p_hT, KD * b)
                    dve.wait_ge(st_h, 16 * b)
                for t in range(TT):
                    last = v.tensor_scalar(h[:, t, :], tile_of(b * TT + t), mvh[:, t, 0:1], rh[:, t:t + 1],
                                           ALU.subtract, ALU.mult)
                last.then_inc(e_h, 1)

            def rows_lower(f):
                for k in range(KD):
                    dve.wait_ge(e_hi, KD * f + k + 1)
                    v.tensor_tensor(hT[1][:, k, :], bank[HT_BANK[k]][:, :], hT[0][:, k, :].bitcast(F32), ALU.subtract).then_inc(e_hT, 1)

            def take_logits(f):
                dve.wait_ge(p_z, f + 1)
                zt = z[:, :, f * TT:(f + 1) * TT] if isinstance(f, int) else z[:, :, bass.ds(f * TT, TT)]
                v.tensor_tensor(zt.rearrange("p e t -> p t e"), zps[:, :, 0:E], bc(eb[:, :].unsqueeze(1), [P, TT, E]), ALU.add).then_inc(e_z, 1)

            def gate(f, half, meanwhile=lambda: None):
                dve.wait_ge(e_th, 2 * f + half + 1)
                v.scalar_tensor_tensor(th[:, half, :], th[:, half, :], 1.0, bank[X2_BANK[half]][:, :], ALU.add, ALU.mult).then_inc(e_u, 1)
                meanwhile()
                settle()
                dve.wait_ge(p_x1, 2 * f + half + 1)
                v.scalar_tensor_tensor(gf[:, half, :], th[:, half, :], 0.5, bank[X1_BANK[half]][:, :], ALU.mult, ALU.mult).then_inc(e_g, 1)

            def gate_lower(f, half):
                dve.wait_ge(e_ghi, 2 * f + half + 1)
                v.tensor_tensor(gT[1][:, half, :], gf[:, half, :], gT[0][:, half, :].bitcast(F32), ALU.subtract).then_inc(e_glo, 1)

            def add_shared(f, t):
                dve.wait_ge(p_y, TT * f + t + 1)
                v.scalar_tensor_tensor(tile_of(f * TT + t), bank[Y_BANK[t]][:, :], gt[:, 1:2], tile_of(f * TT + t),
                                       ALU.mult, ALU.add).then_inc(e_y, 1)

            centre_keys(0)
            dve.wait_ge(ld_xb, 16)
            x_stats(0)
            v.sem_inc(e_stats, 1)
            dve.wait_ge(c_iota, 7)
            v.tensor_copy(pref[:, :, :], prefi[:, :, :])
            v.tensor_copy(row_f[:, :], row_i[:, :])
            v.tensor_copy(tile_f[:, :], tile_i[:, :])
            v.memset(nofirst[:, :, :, :], 1.0)
            settle()
            v.memset(nofirst[:, :, :, 0:1], 0.0)
            dve.wait_ge(ld_rows, 16 * 6)
            dve.wait_ge(c_tanh, 1)
            dve.wait_ge(ld_x[1], 16)
            x_stats(1)
            score_variance(0)
            softmax_inputs(0)
            dve.wait_ge(c_gw, 2)
            v.tensor_tensor(gw[1][:, :, :], gw_raw[:, :, :], gw[0][:, :, :].bitcast(F32), ALU.subtract).then_inc(c_gw, 1)
            for b in (0, 2, 3):
                dve.wait_ge(ld_x[b], 16)
            add_attention(0)
            row_stats(0)
            normalise(0)
            score_variance(1)
            rows_lower(0)
            with dve.Fori(2, NB) as b:
                softmax_inputs(b - 1)
                gate(b - 2, 0)
                take_logits(b - 2)
                add_attention(b - 1)
                centre_keys(b)
                gate_lower(b - 2, 0)
                row_stats(b - 1)
                gate(b - 2, 1)
                normalise(b - 1)
                gate_lower(b - 2, 1)
                x_stats(b)
                score_variance(b)
                for t in range(TT):
                    add_shared(b - 2, t)
                rows_lower(b - 1)
            softmax_inputs(NB - 1)
            gate(NB - 2, 0)
            take_logits(NB - 2)
            add_attention(NB - 1)
            gate_lower(NB - 2, 0)
            gate(NB - 2, 1, lambda: row_stats(NB - 1, [0]))
            row_stats(NB - 1, [1, 2])
            gate_lower(NB - 2, 1)
            row_stats(NB - 1, [3])
            normalise(NB - 1)
            for t in range(TT):
                add_shared(NB - 2, t)
            rows_lower(NB - 1)
            take_logits(NB - 1)
            settle()

            settle()
            v.tensor_scalar(signs[:, :, :], z[:, :, :].bitcast(I32), 31, -2 ** 31, ALU.arith_shift_right, ALU.bitwise_or)
            settle()
            v.tensor_tensor(ordered[:, :, :], z[:, :, :].bitcast(I32), signs[:, :, :], ALU.bitwise_xor)

            def per_token(ap):
                return bc(ap.unsqueeze(1), [P, E, NT])

            def choose(src, dst):
                v.tensor_reduce(m1[:, :], src[:, :, :].rearrange("p e t -> p t e"), AX.X, ALU.max)
                settle()
                v.tensor_tensor(eq[:, :, :], src[:, :, :], per_token(m1[:, :]), ALU.is_equal)
                settle()
                v.tensor_tensor(key[:, :, :], eq[:, :, :], bc(pref[:, :, :], [P, E, NT]), ALU.mult)
                settle()
                v.tensor_reduce(m1[:, :], key[:, :, :].rearrange("p e t -> p t e"), AX.X, ALU.max)
                settle()
                v.tensor_tensor(dst, key[:, :, :], per_token(m1[:, :]), ALU.is_equal)
                settle()

            choose(z, one[:, 0, :, :])
            v.scalar_tensor_tensor(z2[:, :, :], one[:, 0, :, :], -3.0e38, z[:, :, :], ALU.mult, ALU.add)
            settle()
            choose(z2, one[:, 1, :, :])
            v.tensor_tensor(mask[:, :, :], one[:, 0, :, :], one[:, 1, :, :], ALU.add).then_inc(r_one, 1)
            settle()
            v.tensor_tensor(plane[:, :, :, :].rearrange("p l e t -> p l (e t)"),
                            ordered[:, :, :].bitcast(U8).rearrange("p e (t l) -> p l (e t)", l=LEVELS),
                            bc(mask[:, :, :].rearrange("p e t -> p (e t)").unsqueeze(1), [P, LEVELS, E * NT]), ALU.mult)
            settle()
            def per_expert(ap):
                return bc(ap.unsqueeze(2), [P, E, NT])

            def find_digit(r, scores, thresholds, step):
                for half in range(2):
                    ts = slice(half * NT // 2, (half + 1) * NT // 2)
                    v.tensor_tensor(hit[:, :, :, ts], bc(scores[:, :, ts].unsqueeze(2), [P, E, CAND, NT // 2]),
                                    bc(thresholds[:, :, ts].unsqueeze(1), [P, E, CAND, NT // 2]), ALU.is_ge).then_inc(r_hit, 1)
                if r < GATE_ROUNDS:
                    (gate, gate_lower)[r % 2](NB - 1, r // 2)
                else:
                    add_shared(NB - 1, r - GATE_ROUNDS)
                dve.wait_ge(r_cnt, r + 1)
                v.tensor_scalar(reach[:, :, :].rearrange("p e c -> p (e c)"), counts, float(CAP), float(step), ALU.is_ge, ALU.mult)
                settle()
                v.tensor_reduce(digit[:, :], reach[:, :, :], AX.X, ALU.add)
                settle()

            for l in range(LEVELS):
                if l == 0:
                    scores = plane[:, LEVELS - 1, :, :]
                else:
                    v.scalar_tensor_tensor(rest[:, :, :], above_by[:, :, :], 512.0, plane[:, LEVELS - 1 - l, :, :], ALU.mult, ALU.add)
                    settle()
                    scores = rest[:, :, :]
                find_digit(2 * l, scores, high, NIBBLE)
                v.tensor_tensor(rest[:, :, :], scores, per_expert(digit[:, :]), ALU.subtract)
                settle()
                find_digit(2 * l + 1, rest[:, :, :], low, 1)
                if l < LEVELS - 1:
                    v.tensor_tensor(above_by[:, :, :], rest[:, :, :], per_expert(digit[:, :]), ALU.subtract)
                    settle()
            v.tensor_tensor(flags[:, 0, :, :], rest[:, :, :], per_expert(digit[:, :]), ALU.is_gt)
            v.tensor_tensor(flags[:, 1, :, :], rest[:, :, :], per_expert(digit[:, :]), ALU.is_equal).then_inc(r_flags, 1)

            def flat(ap):
                return ap.rearrange("p a e t -> p (a e t)")

            dve.wait_ge(r_flagsP, 1)
            v.tensor_tensor_scan(flat(cum[:, :, :, :]), flat(nofirst[:, :, :, :]), total_ps, 0.0, ALU.mult, ALU.add)
            settle()
            v.tensor_tensor(flat(rank[:, :, :, :]), flat(cum[:, :, :, :]), prefix_ps, ALU.add)
            v.tensor_scalar(room[:, :], cum[:, 0, :, NT - 1], -1.0, float(CAP), ALU.mult, ALU.add)
            settle()
            v.tensor_tensor(before[:, :, :], rank[:, 1, :, :], per_expert(room[:, :]), ALU.min)
            v.tensor_tensor(fits[:, :, :], rank[:, 1, :, :], per_expert(room[:, :]), ALU.is_lt)
            settle()
            v.tensor_tensor(slot[:, :, :], rank[:, 0, :, :], before[:, :, :], ALU.add)
            v.tensor_tensor(fits[:, :, :], fits[:, :, :], flags[:, 1, :, :], ALU.mult)
            settle()
            v.tensor_scalar(slf[:, :, :], slot[:, :, :], P - 1, None, ALU.bitwise_and)
            v.tensor_scalar(slg[:, :, :], slot[:, :, :], 7, None, ALU.logical_shift_right)
            v.tensor_tensor(kept[:, :, :], fits[:, :, :], flags[:, 0, :, :], ALU.add)
            settle()
            v.scalar_tensor_tensor(row1[:, :, :], slf[:, :, :], 1.0, kept[:, :, :], ALU.add, ALU.mult)
            v.tensor_copy(slgf[:, :, :], slg[:, :, :])
            settle()
            v.tensor_tensor(rowc[:, :, :, :], one[:, :, :, :], bc(row1[:, :, :].unsqueeze(1), [P, 2, E, NT]), ALU.mult)
            v.tensor_tensor(ing[:, :, :], bc(slgf[:, :, :].rearrange("p e t -> p (e t)").unsqueeze(1), [P, GE, E * NT]),
                            group[:, :, :], ALU.is_equal)
            settle()
            v.tensor_reduce(srow[:, :, :], rowc[:, :, :, :].rearrange("p c e t -> p c t e"), AX.X, ALU.max)
            dve.wait_ge(r_told, 1)
            v.tensor_tensor(place[:, :, :, :], bc(told[:, :, :].unsqueeze(2), [P, 2 * NV, GE, E * NT]),
                            bc(ing[:, :, :].unsqueeze(1), [P, 2 * NV, GE, E * NT]), ALU.mult)
            settle()
            for c in range(2):
                v.tensor_tensor(hot[:, c, :, :], bc(srow[:, c:c + 1, :], [P, P, NT]), iota_s[:, :, :],
                                ALU.is_equal).then_inc(r_hot, 1)
            dve.wait_ge(r_slot, 1)
            v.tensor_copy(slots[:, :, :].rearrange("p n g -> p (n g)"), slots_ps)
            settle()
            v.scalar_tensor_tensor(tok[:, :], slots[:, 0, :], float(P), slots[:, 1, :], ALU.mult, ALU.add).then_inc(r_idx, 1)
            v.tensor_tensor(wsum[:, :], slots[:, 2, :], slots[:, 3, :], ALU.add)
            settle()
            v.tensor_tensor(wslot[:, :], wsum[:, :], slots[:, 4, :], ALU.add).then_inc(r_weight, 1)

            def gathered_lower(e):
                for k in range(KD):
                    dve.wait_ge(f_hi, KD * e + k + 1)
                    v.tensor_tensor(hgT[1][:, k, :], bank[k][:, 0:CAP], hgT[0][:, k, :].bitcast(F32), ALU.subtract).then_inc(f_hgT, 1)

            def lower_w1(n, w1, k):
                dve.wait_ge(w1_hi, W1N * n + k + 1)
                v.tensor_tensor(w1[1][:, k, :], w1_raw[:, k, :], w1[0][:, k, :].bitcast(F32), ALU.subtract).then_inc(w1_lo, 1)

            def lower_w2(n, w2, k):
                dve.wait_ge(w2_hi, W2N * n + k + 1)
                v.tensor_tensor(w2[1][:, k, :], w2_raw[:, k, :], w2[0][:, k, :].bitcast(F32), ALU.subtract).then_inc(w2_lo, 1)

            def routed_gate(e, half):
                dve.wait_ge(f_th, 2 * e + half + 1)
                v.scalar_tensor_tensor(th[:, half, 0:CAP], th[:, half, 0:CAP], 1.0, bank[4 + 2 * half][:, 0:CAP],
                                       ALU.add, ALU.mult)
                settle()
                dve.wait_ge(q_x1, 2 * e + half + 1)
                v.scalar_tensor_tensor(gf[:, half, 0:CAP], th[:, half, 0:CAP], 0.5, bank[5 + 2 * half][:, 0:CAP],
                                       ALU.mult, ALU.mult).then_inc(f_g, 1)

            def routed_gate_lower(e, half):
                dve.wait_ge(f_ghi, 2 * e + half + 1)
                v.tensor_tensor(gT[1][:, half, 0:CAP], gf[:, half, 0:CAP], gT[0][:, half, 0:CAP].bitcast(F32),
                                ALU.subtract).then_inc(f_glo, 1)

            def expert(e, par):
                last = isinstance(e, int) and e == E - 1
                gathered_lower(e)
                if not last:
                    for k in range(KD - 1):
                        lower_w1(e + 2, w1r[1 - par], k)
                routed_gate(e, 0)
                if not last:
                    lower_w1(e + 2, w1r[1 - par], KD - 1)
                routed_gate_lower(e, 0)
                routed_gate(e, 1)
                if not last:
                    lower_w2(e + 2, w2r[1 - par], 0)
                routed_gate_lower(e, 1)
                if not last:
                    lower_w2(e + 2, w2r[1 - par], 1)

            dve.wait_ge(w2_lo, 2 * W2N)
            expert(0, 0)
            with dve.Fori(1, E - 2, 2) as e:
                expert(e, 1)
                expert(e + 1, 0)
            expert(E - 2, 1)
            expert(E - 1, 0)


_INS = ["x", "ctx_512", "g_xattn", "g_ffn", "L0_xattn_W_k", "L0_xattn_b_k", "L0_xattn_ln_gamma",
        "L0_xattn_ln_beta", "L0_ffn_gate_w", "L0_ffn_expert_bias", "L0_ffn_shared_w1",
        "L0_ffn_shared_w2", "L0_ffn_routed_w1", "L0_ffn_routed_w2"]


def kernel(**inputs):
    import concourse.bacc as bacc
    from concourse.bass_utils import run_bass_kernel_spmd

    nc = bacc.Bacc("TRN2", target_bir_lowering=False, num_devices=1)
    arrays, args = {}, []
    for name in _INS:
        a = np.ascontiguousarray(inputs[name])
        arrays[f"in_{name}"] = a
        args.append(nc.dram_tensor(f"in_{name}", a.shape, mybir.dt.from_np(a.dtype), kind="ExternalInput").ap())
    args.append(nc.dram_tensor("out_0", (NB, S, D), F32, kind="ExternalOutput").ap())
    build(nc, *args)
    r = run_bass_kernel_spmd(nc, [arrays], core_ids=[0])
    return r.results[0]["out_0"]
```
